# Optimizing a Trainium2 kernel written in Bass

```python
import numpy as np
import jax
import jax.numpy as jnp

def _softmax(x, axis=-1):
    return jax.nn.softmax(x, axis=axis)

def _gelu(x):
    return jax.nn.gelu(x, approximate=True)

def _silu(x):
    return jax.nn.silu(x)

def _sigmoid(x):
    return jax.nn.sigmoid(x)

def _layernorm(x, axis=-1, eps=1e-05):
    m = jnp.mean(x, axis=axis, keepdims=True)
    v = jnp.var(x, axis=axis, keepdims=True)
    return (x - m) / jnp.sqrt(v + eps)

def _scatter_add(tgt, idx, src, axis=0):
    return tgt.at[idx].add(src)

def _segment_sum(src, seg, n):
    return jax.ops.segment_sum(src, seg, n)
kernel_name = 'mk_prb_d1_jaxref_r8_58298f'

def setup_inputs(seed: int=0):
    np.random.seed(seed)
    _w = jnp.asarray

    def _L0_attn_setup():
        import jax, jax.numpy as jnp
        import numpy as np
        N_HEAD = 16
        key = jax.random.key(seed)
        k1, k2, k3, k4, k5 = jax.random.split(key, 5)
        B, T, C = (8, 256, 128)
        hs = C // N_HEAD
        return {'ids': jax.random.normal(k1, (B, T, C), dtype=jnp.float32), 'qkv_w': jax.random.normal(k2, (3 * hs, C), dtype=jnp.float32) * C ** (-0.5), 'qkv_b': jax.random.normal(k3, (3 * hs,), dtype=jnp.float32) * 0.02, 'proj_w': jax.random.normal(k4, (C, C), dtype=jnp.float32) * C ** (-0.5), 'proj_b': jax.random.normal(k5, (C,), dtype=jnp.float32) * 0.02}
    _L0_attn_in = _L0_attn_setup()

    def _L0_ffn_setup():
        import jax, jax.numpy as jnp
        import numpy as np
        B, T, D, FF, E, TOP_K = (4, 256, 128, 512, 8, 2)
        key = jax.random.key(seed)
        k0, k1, k2, k3 = jax.random.split(key, 4)
        x = jax.random.normal(k0, (B, T, D), dtype=jnp.float32)
        router_w = jax.random.normal(k1, (E, D), dtype=jnp.float32) * D ** (-0.5)
        w1 = jax.random.normal(k2, (E, D, FF), dtype=jnp.float32) * D ** (-0.5)
        w2 = jax.random.normal(k3, (E, FF, D), dtype=jnp.float32) * FF ** (-0.5)
        return {'x': x, 'router_w': router_w, 'w1': w1, 'w2': w2}
    _L0_ffn_in = _L0_ffn_setup()
    _d = {'L0_attn_ids': _L0_attn_in['ids'], 'L0_attn_qkv_w': _L0_attn_in['qkv_w'], 'L0_attn_qkv_b': _L0_attn_in['qkv_b'], 'L0_attn_proj_w': _L0_attn_in['proj_w'], 'L0_attn_proj_b': _L0_attn_in['proj_b'], 'L0_ffn_router_w': _L0_ffn_in['router_w'], 'L0_ffn_w1': _L0_ffn_in['w1'], 'L0_ffn_w2': _L0_ffn_in['w2']}
    _x0 = _d['L0_attn_ids']
    _d['L0_attn_ids'] = jax.random.normal(jax.random.fold_in(jax.random.key(seed), 1), (16, 256, 128), dtype=_x0.dtype)
    del _x0
    return _d

def reference(L0_attn_ids, L0_attn_qkv_w, L0_attn_qkv_b, L0_attn_proj_w, L0_attn_proj_b, L0_ffn_router_w, L0_ffn_w1, L0_ffn_w2):

    def _L0_attn_ref(ids, qkv_w, qkv_b, proj_w, proj_b):
        import jax, jax.numpy as jnp
        import numpy as np
        N_HEAD = 16
        B, T, C = ids.shape
        hs = qkv_w.shape[0] // 3
        qkv = ids @ qkv_w.T + qkv_b
        q, k, v = jnp.split(qkv, 3, axis=-1)
        wei = jnp.einsum('btd,bsd->bts', q, k)
        tril = jnp.tril(jnp.ones((T, T), dtype=bool))
        wei = jnp.where(tril, wei, jnp.float32(0.0))
        out_h = jnp.einsum('bts,bsd->btd', wei, v)
        out = jnp.tile(out_h, (1, 1, N_HEAD))
        return out @ proj_w.T + proj_b

    def _L0_ffn_ref(x, router_w, w1, w2):
        import jax, jax.numpy as jnp
        import numpy as np
        B, T, D, FF, E, TOP_K = (4, 256, 128, 512, 8, 2)
        b, t, d = x.shape
        e, k = (router_w.shape[0], TOP_K)
        xf = x.reshape(-1, d)
        n = xf.shape[0]
        logits = xf @ router_w.T
        topv, topi = jax.lax.top_k(logits, k)
        topw = jax.nn.softmax(topv.astype(jnp.float32), axis=-1).astype(x.dtype)
        idx_flat = topi.reshape(-1)
        w_flat = topw.reshape(-1)
        sort_idx = jnp.argsort(idx_flat)
        src = jnp.repeat(jnp.arange(n), k)
        rev = src[sort_idx]
        sw = w_flat[sort_idx]
        perm = xf[rev]
        chunks = perm.reshape(e, n * k // e, d)
        h = jax.nn.gelu(jnp.einsum('ecd,edf->ecf', chunks, w1), approximate=False)
        y = jnp.einsum('ecf,efd->ecd', h, w2).reshape(n * k, d)
        y = y * sw[:, None]
        out = jnp.zeros((n, d), dtype=x.dtype).at[rev].add(y)
        return out.reshape(b, t, d)
    x = L0_attn_ids
    xn = _layernorm(x, axis=-1)
    x = x + _L0_attn_ref(xn, L0_attn_qkv_w, L0_attn_qkv_b, L0_attn_proj_w, L0_attn_proj_b) + _L0_ffn_ref(xn, L0_ffn_router_w, L0_ffn_w1, L0_ffn_w2)
    return x

_drawn_inputs = setup_inputs


def setup_inputs(seed=0):
    import zlib

    import numpy as np

    out = dict(_drawn_inputs(seed))
    spreads = {}
    factors = {'L0_attn_proj_b': 198.065,
     'L0_ffn_router_w': 8.0,
     'L0_ffn_w1': 7.826,
     'L0_ffn_w2': 7.146,
     'L0_attn_qkv_b': 2.726}
    for name, (base, spread) in spreads.items():
        noise = np.random.default_rng([zlib.crc32(name.encode()), seed]).standard_normal(out[name].shape)
        drawn = base * np.exp(spread * noise) if base else spread * noise
        out[name] = jnp.asarray(drawn.astype(out[name].dtype))
    for name, factor in factors.items():
        out[name] = (out[name] * factor).astype(out[name].dtype)
    return out
```

```python
from contextlib import ExitStack

import concourse.bass as bass
from concourse import mybir

ALU = mybir.AluOpType
ACT = mybir.ActivationFunctionType
AX = mybir.AxisListType
F32 = mybir.dt.float32
BF16 = mybir.dt.bfloat16
I32 = mybir.dt.int32
U32 = mybir.dt.uint32

P = 128
EPS = 1e-5
FILL = -3.0e38


class Steps:

    def __init__(self, engine, semaphore):
        self.engine, self.semaphore, self.count, self.base = engine, semaphore, 0, 0

    def end(self, instruction):
        instruction.then_inc(self.semaphore, 1)
        self.count += 1

    def settle(self):
        self.engine.wait_ge(self.semaphore, self.base + self.count)


def layer_program(nc, ids, qkv_w, qkv_b, proj_w, proj_b, router_w, w1, w2, out):
    B, T, D = ids.shape
    HS = qkv_w.shape[0] // 3
    NH = D // HS
    E, _, FF = w1.shape
    N = B * T
    NT = N // P
    TG = 4
    NG = NT // TG
    ITEMS = 2 * NT
    CT = ITEMS // E
    HALF = 512
    HT = HALF // P
    FC = FF // P
    BT = T // P
    assert D == P and T == 2 * P and NG == E and B == 2 * E and CT * P == 2 * HALF and HS == 8 and E == 8

    x_rows = ids.rearrange("b t d -> (b t) d").rearrange("(i p) d -> p i d", p=P)
    out_rows = out.rearrange("b t d -> (b t) d").rearrange("(i p) d -> p i d", p=P)
    xn_dram = nc.dram_tensor("xn_scratch", [N, D], F32).ap()
    xn_rows = xn_dram.rearrange("(i p) d -> p i d", p=P)
    y_dram = nc.dram_tensor("y_scratch", [2 * N, D], F32).ap()
    y_rows = y_dram.rearrange("(j p) d -> p j d", p=P)
    w1_rows = w1.rearrange("e d f -> d e f")
    w2_rows = w2.rearrange("e (c p) d -> p e c d", p=P)

    with ExitStack() as ctx:
        def sb(name, shape, dt=F32):
            return ctx.enter_context(nc.sbuf_tensor(name, shape, dt))

        def sem(name):
            return ctx.enter_context(nc.semaphore(name))

        bank = [ctx.enter_context(nc.psum_tensor(f"bank{n}", [P, 512], F32)) for n in range(8)]
        turn_ps, mid_ps, y_ps = bank[0:2], bank[2:4], bank[4:6]
        wei_ps, att_ps = bank[6], bank[7]

        x_all = sb("x_all", [P, NT, D])
        base = sb("base", [P, NT, D])
        qk_t = sb("qk_t", [32 + HS, N])
        lv = sb("lv", [P, NT, 2 * HS])
        stats = sb("stats", [P, 2, TG, 6])
        mv = sb("mv", [P, 2, TG, 2])
        var_eps = sb("var_eps", [P, 2, TG])
        power = sb("power", [P, TG])
        rstd = sb("rstd", [P, 2, TG])
        xn = sb("xn", [P, 4, TG, D])
        xn_t = sb("xn_t", [P, 2, TG * P])
        w_in = sb("w_in", [80, D])
        w_in_t = sb("w_in_t", [P, 80])
        qk_bias = sb("qk_bias", [32 + HS, 1])
        v_bias = sb("v_bias", [P, HS])
        proj_in = sb("proj_in", [P, D])
        proj_sum = sb("proj_sum", [P, HS])
        proj_t = sb("proj_t", [HS + 1, D])
        ident = sb("ident", [P, P])
        causal = sb("causal", [P, 3, P])
        not_before = sb("not_before", [P, P], BF16)
        ones = sb("ones", [P, P], BF16)
        ramp = sb("ramp", [P, P], BF16)
        lane = sb("lane", [P, 1])
        prefer = sb("prefer", [P, E])
        best = sb("best", [P, 2, NT])
        hit = sb("hit", [P, NT, E])
        hit_rank = sb("hit_rank", [P, NT])
        choice = sb("choice", [P, 2, NT, E])
        rest = sb("rest", [P, NT, E])
        chosen = sb("chosen", [P, E * NT], BF16)
        through = sb("through", [P, E * NT])
        place = sb("place", [P, E * NT])
        zeros = sb("zeros", [P, E * NT])
        pos = sb("pos", [P, ITEMS])
        pos_i = sb("pos_i", [P, ITEMS], I32)
        lo_i = sb("lo_i", [P, ITEMS], I32)
        hi_i = sb("hi_i", [P, ITEMS], I32)
        lo = sb("lo", [P, ITEMS])
        hi = sb("hi", [P, ITEMS], BF16)
        lo_hot = sb("lo_hot", [P, ITEMS, P], BF16)
        hi_hot = sb("hi_hot", [P, ITEMS, 64], BF16)
        hi_val = sb("hi_val", [P, ITEMS, 2, 64], BF16)
        part = sb("part", [P, 2, ITEMS])
        item = sb("item", [P, ITEMS])
        second = sb("second", [P, ITEMS])
        item_u = sb("item_u", [P, ITEMS], U32)
        token_u = sb("token_u", [P, ITEMS], U32)
        gap = sb("gap", [P, NT])
        weight = sb("weight", [P, 2, NT])
        wsum = sb("wsum", [P, NT])
        w1_s = [sb(f"w1_s{s}", [P, FF]) for s in range(2)]
        w2_s = [sb(f"w2_s{s}", [P, FC, D]) for s in range(2)]
        token_s = [sb(f"token_s{s}", [P, CT], U32) for s in range(2)]
        item_s = [sb(f"item_s{s}", [P, CT], U32) for s in range(2)]
        rows_s = [sb(f"rows_s{s}", [P, CT, D]) for s in range(2)]
        rows_t = sb("rows_t", [P, 2, HALF])
        mid = sb("mid", [P, FC, HALF])
        y_t = sb("y_t", [P, 2, HALF])
        y_s = [sb(f"y_s{s}", [P, CT, D]) for s in range(2)]
        k_s = [sb(f"k_s{s}", [HS, T]) for s in range(2)]
        v_s = [sb(f"v_s{s}", [P, BT, HS]) for s in range(2)]
        wei_s = [sb(f"wei_s{s}", [P, 3 * P]) for s in range(2)]
        att_s = [sb(f"att_s{s}", [HS + 1, T]) for s in range(2)]
        y_in = sb("y_in", [P, 4, 2, TG, D])

        x_in = [sem(f"x_in{g}") for g in range(NG)]
        x_ready = sem("x_ready")
        w_in_zero = sem("w_in_zero")
        w_in_in = sem("w_in_in")
        small_in = sem("small_in")
        proj_loaded = sem("proj_loaded")
        consts = sem("consts")
        pool_step = sem("pool_step")
        dve_step = sem("dve_step")
        held = sem("held")
        var_ready = sem("var_ready")
        rstd_ready = sem("rstd_ready")
        xn_ready = sem("xn_ready")
        xn_free = sem("xn_free")
        xn_stored = [sem(f"xn_stored{s}") for s in range(4)]
        w_in_turned = sem("w_in_turned")
        w_in_ready = sem("w_in_ready")
        proj_summed = sem("proj_summed")
        proj_turned = sem("proj_turned")
        proj_ready = sem("proj_ready")
        xn_turned = sem("xn_turned")
        xn_t_ready = sem("xn_t_ready")
        lv_done = sem("lv_done")
        qk_done = sem("qk_done")
        front_out = sem("front_out")
        chosen_ready = sem("chosen_ready")
        counted = sem("counted")
        gap_ready = sem("gap_ready")
        gap_exp = sem("gap_exp")
        lo_ready = sem("lo_ready")
        hi_ready = sem("hi_ready")
        listed = sem("listed")
        list_ready = sem("list_ready")
        w_loaded = [sem(f"w_loaded{s}") for s in range(2)]
        gathered = [[sem(f"gathered{s}{c}") for c in range(2)] for s in range(2)]
        scattered = [sem(f"scattered{s}") for s in range(2)]
        rows_turned = sem("rows_turned")
        rows_t_ready = sem("rows_t_ready")
        mid_done = sem("mid_done")
        mid_ready = sem("mid_ready")
        y_t_done = sem("y_t_done")
        y_t_ready = sem("y_t_ready")
        y_turned = sem("y_turned")
        y_ready = sem("y_ready")
        y_free = sem("y_free")
        kv_ready = sem("kv_ready")
        wei_done = sem("wei_done")
        wei_ready = sem("wei_ready")
        heads_done = sem("heads_done")
        heads_ready = sem("heads_ready")
        att_done = sem("att_done")
        base_ready = sem("base_ready")
        y_in_sem = [sem(f"y_in_sem{s}") for s in range(4)]
        y_back = sem("y_back")
        combined = sem("combined")
        out_stored = sem("out_stored")

        block = ctx.enter_context(nc.Block())

        @block.sync
        def _(sp):
            for g in range(2):
                sp.dma_start(x_all[:, g * TG:(g + 1) * TG, :], x_rows[:, g * TG:(g + 1) * TG, :]).then_inc(x_in[g], 16)
            sp.wait_ge(w_in_zero, 1)
            sp.dma_start(w_in[0:HS, :], qkv_w[0:HS, :]).then_inc(w_in_in, 16)
            sp.dma_start(w_in[32:32 + HS, :], qkv_w[HS:2 * HS, :]).then_inc(w_in_in, 16)
            sp.dma_start(w_in[64:64 + E, :], router_w).then_inc(w_in_in, 16)
            sp.dma_start(w_in[64 + E:64 + E + HS, :], qkv_w[2 * HS:3 * HS, :]).then_inc(w_in_in, 16)
            for g in range(2, NG):
                sp.dma_start(x_all[:, g * TG:(g + 1) * TG, :], x_rows[:, g * TG:(g + 1) * TG, :]).then_inc(x_in[g], 16)
            for s in range(2):
                sp.dma_start(w1_s[s][:], w1_rows[:, s, :]).then_inc(w_loaded[s], 16)
                sp.dma_start(w2_s[s][:], w2_rows[:, s, :, :]).then_inc(w_loaded[s], 16)
            for g in range(NG):
                sp.wait_ge(x_in[g], 16)
                sp.sem_inc(x_ready, 1)
            with sp.Fori(0, E // 2 - 1) as it:
                for s in range(2):
                    e = it * 2 + (2 + s)
                    sp.wait_ge(y_t_done, it * 4 + (2 + 2 * s))
                    sp.dma_start(w1_s[s][:], w1_rows[:, bass.ds(e, 1), :]).then_inc(w_loaded[s], 16)
                    sp.dma_start(w2_s[s][:], w2_rows[:, bass.ds(e, 1), :, :]).then_inc(w_loaded[s], 16)
            for s in range(2):
                sp.wait_ge(scattered[s], 16 * CT * E // 2)

            def read_back(g):
                for k in range(2):
                    sp.dma_start(y_in[:, g % 4, k, :, :],
                                 y_rows[:, k * NT + g * TG:k * NT + (g + 1) * TG, :]).then_inc(y_in_sem[g % 4], 16)

            for g in range(4):
                read_back(g)
            for g in range(NG):
                sp.wait_ge(y_in_sem[g % 4], 32 * (g // 4 + 1))
                sp.sem_inc(y_back, 1)
                if g + 4 < NG:
                    sp.wait_ge(combined, g + 1)
                    read_back(g + 4)

        @block.gpsimd
        def _(pool):
            step = Steps(pool, pool_step)
            nc.gpsimd.memset(w_in[:], 0.0).then_inc(w_in_zero, 1)
            nc.gpsimd.memset(qk_bias[:], 0.0)
            nc.gpsimd.memset(power[:], -0.5)
            nc.gpsimd.memset(ident[:], 0.0)
            nc.gpsimd.memset(causal[:], 1.0)
            nc.gpsimd.memset(not_before[:], -1.0)
            nc.gpsimd.memset(ones[:], 1.0)
            for s in range(2):
                nc.gpsimd.memset(att_s[s][:], 1.0)
            step.end(nc.gpsimd.memset(zeros[:], 0.0))
            step.settle()
            nc.gpsimd.affine_select(out=ident[:], in_=ident[:], compare_op=ALU.not_equal, fill=1.0, base=0,
                                    pattern=[[-1, P]], channel_multiplier=1).then_inc(consts, 1)
            for b in (0, 2):
                nc.gpsimd.affine_select(out=causal[:, b, :], in_=causal[:, b, :], compare_op=ALU.is_ge, fill=0.0,
                                        base=0, pattern=[[1, P]], channel_multiplier=-1)
            nc.gpsimd.affine_select(out=not_before[:], in_=not_before[:], compare_op=ALU.is_ge, fill=0.0,
                                    base=0, pattern=[[-1, P]], channel_multiplier=1)
            nc.gpsimd.iota(ramp[:], [[1, P]], base=0, channel_multiplier=0, allow_small_or_imprecise_dtypes=True)
            nc.gpsimd.iota(lane[:], [[0, 1]], base=0, channel_multiplier=1, allow_small_or_imprecise_dtypes=True)
            nc.gpsimd.iota(prefer[:], [[-1, E]], base=E, channel_multiplier=0,
                           allow_small_or_imprecise_dtypes=True).then_inc(consts, 1)
            pool.sem_inc(xn_free, 4)
            for g in range(NG + 1):
                if g < NG:
                    pool.wait_ge(var_ready, g + 1)
                    nc.gpsimd.tensor_tensor(rstd[:, g % 2, :], var_eps[:, g % 2, :], power[:], ALU.pow).then_inc(rstd_ready, 1)
                if g >= 1:
                    pool.wait_ge(xn_ready, g)
                    pool.dma_start(xn_rows[:, (g - 1) * TG:g * TG, :], xn[:, (g - 1) % 4, :, :]).then_inc(xn_stored[(g - 1) % 4], 16)
                if g >= 3:
                    pool.wait_ge(xn_stored[(g - 3) % 4], 16 * ((g - 3) // 4 + 1))
                    pool.wait_ge(xn_turned, g - 2)
                    pool.sem_inc(xn_free, 1)
            for g in (NG - 2, NG - 1):
                pool.wait_ge(xn_stored[g % 4], 16 * (g // 4 + 1))
            pool.sem_inc(y_free, 2)

            def gather(e, s):
                step.end(nc.gpsimd.tensor_copy(token_s[s][:], token_u[:, bass.ds(e * CT, CT)]))
                step.settle()
                pool.sem_inc(held, 1)
                for t in range(CT):
                    nc.gpsimd.indirect_dma_start(
                        out=rows_s[s][:, t, :], out_offset=None, in_=xn_dram,
                        in_offset=bass.IndirectOffsetOnAxis(ap=token_s[s][:, t:t + 1], axis=0),
                    ).then_inc(gathered[s][t // HT], 16)

            def scatter(e, s):
                step.end(nc.gpsimd.tensor_copy(item_s[s][:], item_u[:, bass.ds(e * CT, CT)]))
                step.settle()
                for c in range(2):
                    pool.wait_ge(y_ready, e * 2 + (c + 3))
                    pool.sem_inc(held, 1)
                    for t in range(c * HT, (c + 1) * HT):
                        nc.gpsimd.indirect_dma_start(
                            out=y_dram, out_offset=bass.IndirectOffsetOnAxis(ap=item_s[s][:, t:t + 1], axis=0),
                            in_=y_s[s][:, t, :], in_offset=None,
                        ).then_inc(scattered[s], 16)

            def confirm(e_scatters, s):
                pool.wait_ge(scattered[s], e_scatters)
                pool.sem_inc(y_free, 1)

            pool.wait_ge(list_ready, 1)
            gather(0, 0)
            gather(1, 1)
            scatter(0, 0)
            start = step.count
            with pool.Fori(0, E // 2 - 1) as it:
                step.base = it * 4
                for s in range(2):
                    e = it * 2 + (1 + s)
                    pool.wait_ge(rows_turned, e * 2)
                    gather(e + 1, s)
                    confirm((it + 1) * (16 * CT), s)
                    scatter(e, 1 - s)
                assert step.count == start + 4
            step.base, step.count = 0, start + 4 * (E // 2 - 1)
            scatter(E - 1, 1)

        @block.scalar
        def _(act):
            act.dma_start(proj_in[:], proj_w).then_inc(proj_loaded, 16)
            act.wait_ge(consts, 1)
            act.dma_start(qk_bias[0:HS, :], qkv_b[0:HS].unsqueeze(1)).then_inc(small_in, 16)
            act.dma_start(qk_bias[32:32 + HS, :], qkv_b[HS:2 * HS].unsqueeze(1)).then_inc(small_in, 16)
            act.dma_start(v_bias[:], qkv_b[2 * HS:3 * HS].partition_broadcast(P)).then_inc(small_in, 16)
            act.dma_start(proj_t[HS:HS + 1, :], proj_b.unsqueeze(0)).then_inc(small_in, 16)
            act.wait_ge(w_in_turned, 1)
            nc.scalar.copy(w_in_t[:], turn_ps[0][:, 0:80]).then_inc(w_in_ready, 1)
            act.wait_ge(proj_turned, 1)
            nc.scalar.copy(proj_t[0:HS, :], turn_ps[1][0:HS, 0:P]).then_inc(proj_ready, 1)
            act.wait_ge(small_in, 64)
            act.sem_inc(front_out, 4)
            with act.Fori(0, NG // 2) as it:
                for s in range(2):
                    act.wait_ge(xn_turned, it * 2 + (s + 1))
                    nc.scalar.copy(xn_t[:, s, :], turn_ps[s][:]).then_inc(xn_t_ready, 1)
                for s in range(2):
                    g = it * 2 + s
                    act.wait_ge(lv_done, it * 2 + (s + 1))
                    nc.scalar.copy(lv[:, bass.ds(g * TG, TG), :],
                                   y_ps[s][:, 0:TG * 2 * HS].rearrange("p (t c) -> p t c", t=TG)).then_inc(front_out, 1)
                    act.wait_ge(qk_done, it * 2 + (s + 1))
                    nc.scalar.activation(qk_t[:, bass.ds(g * (TG * P), TG * P)], mid_ps[s][0:32 + HS, :],
                                         ACT.Identity, bias=qk_bias[:, 0:1]).then_inc(front_out, 1)
            act.wait_ge(gap_ready, 1)
            nc.scalar.activation(gap[:], gap[:], ACT.Exp).then_inc(gap_exp, 1)

            with act.Fori(0, E) as e:
                for c in range(2):
                    act.wait_ge(rows_turned, e * 2 + (c + 1))
                    nc.scalar.copy(rows_t[:, c, :], turn_ps[c][:]).then_inc(rows_t_ready, 1)
                for c in range(2):
                    for f in range(FC):
                        act.wait_ge(mid_done, e * (2 * FC) + (c * FC + f + 1))
                        nc.scalar.activation(mid[:, f, :], mid_ps[f % 2][:], ACT.Gelu).then_inc(mid_ready, 1)

            for g in range(NG):
                act.wait_ge(combined, g + 1)
                act.dma_start(out_rows[:, g * TG:(g + 1) * TG, :], base[:, g * TG:(g + 1) * TG, :]).then_inc(out_stored, 16)
            act.wait_ge(out_stored, 16 * NG)

        @block.vector
        def _(dve):
            step = Steps(dve, dve_step)
            dve.wait_ge(proj_loaded, 16)
            nc.vector.tensor_reduce(proj_sum[:], proj_in[:].rearrange("c (h d) -> c d h", h=NH), AX.X,
                                    ALU.add).then_inc(proj_summed, 1)

            start = step.count
            with dve.Fori(0, NG // 4) as it:
                step.base = it * 4
                for pair in range(2):
                    for r in range(2):
                        s = 2 * pair + r
                        g = it * 4 + s
                        dve.wait_ge(x_ready, it * 4 + (s + 1))
                        for t in range(TG):
                            last = nc.vector.bn_stats(stats[:, r, t, :], x_all[:, bass.ds(g * TG + t, 1), :].squeeze(1))
                        dve.drain()
                        for t in range(TG):
                            last = nc.vector.bn_aggr(mv[:, r, t, :], stats[:, r, t, :])
                        step.end(last)
                        step.settle()
                        nc.vector.tensor_scalar(var_eps[:, r, :], mv[:, r, :, 1], EPS, None, ALU.add).then_inc(var_ready, 1)
                    for r in range(2):
                        s = 2 * pair + r
                        g = it * 4 + s
                        dve.wait_ge(rstd_ready, it * 4 + (s + 1))
                        dve.wait_ge(xn_free, it * 4 + (s + 1))
                        for t in range(TG):
                            last = nc.vector.tensor_scalar(xn[:, s, t, :], x_all[:, bass.ds(g * TG + t, 1), :].squeeze(1),
                                                           mv[:, r, t, 0:1], rstd[:, r, t:t + 1], ALU.subtract, ALU.mult)
                        last.then_inc(xn_ready, 1)
                assert step.count == start + 4
            step.base, step.count = 0, start + 4 * (NG // 4)

            dve.wait_ge(consts, 2)
            dve.wait_ge(front_out, 4 + 2 * NG)
            logits = lv[:, :, 0:E]
            per_token = [P, NT, E]
            for k, left in enumerate((logits, rest[:])):
                step.end(nc.vector.tensor_reduce(best[:, k, :], left, AX.X, ALU.max))
                step.settle()
                step.end(nc.vector.tensor_tensor(hit[:], left, best[:, k, :].unsqueeze(2).to_broadcast(per_token),
                                                 ALU.is_equal))
                step.settle()
                step.end(nc.vector.tensor_tensor(hit[:], hit[:], prefer[:].unsqueeze(1).to_broadcast(per_token),
                                                 ALU.mult))
                step.settle()
                step.end(nc.vector.tensor_reduce(hit_rank[:], hit[:], AX.X, ALU.max))
                step.settle()
                step.end(nc.vector.tensor_tensor(choice[:, k, :, :], hit[:],
                                                 hit_rank[:].unsqueeze(2).to_broadcast(per_token), ALU.is_equal))
                step.settle()
                if k == 0:
                    step.end(nc.vector.scalar_tensor_tensor(rest[:], choice[:, 0, :, :], FILL, logits, ALU.mult,
                                                            ALU.add))
                    step.settle()
            nc.vector.tensor_tensor(chosen[:].rearrange("p (e i) -> p i e", e=E), choice[:, 0, :, :], choice[:, 1, :, :], ALU.add).then_inc(chosen_ready, 1)
            nc.vector.tensor_tensor(gap[:], best[:, 1, :], best[:, 0, :], ALU.subtract).then_inc(gap_ready, 1)

            dve.wait_ge(counted, 1)
            step.end(nc.vector.tensor_tensor_scan(through[:], att_ps[:, 0:NT * E],
                                                  zeros[:], 0.0, ALU.add, ALU.add))
            step.settle()
            step.end(nc.vector.tensor_tensor(place[:], through[:], wei_ps[:, 0:NT * E], ALU.add))
            step.settle()
            by_expert = place[:].rearrange("p (e i) -> p i e", e=E)
            for k in range(2):
                step.end(nc.vector.tensor_tensor(hit[:], choice[:, k, :, :], by_expert, ALU.mult))
                step.settle()
                step.end(nc.vector.tensor_reduce(pos[:, k * NT:(k + 1) * NT], hit[:], AX.X, ALU.add))
                step.settle()
            step.end(nc.vector.tensor_copy(pos_i[:], pos[:]))
            step.settle()
            nc.vector.tensor_scalar(lo_i[:], pos_i[:], P - 1, None, ALU.bitwise_and)
            step.end(nc.vector.tensor_scalar(hi_i[:], pos_i[:], 7, None, ALU.logical_shift_right))
            step.settle()
            nc.vector.tensor_copy(lo[:], lo_i[:])
            step.end(nc.vector.tensor_copy(hi[:], hi_i[:]))
            step.settle()
            step.end(nc.vector.tensor_tensor(hi_hot[:], ramp[:, 0:64].unsqueeze(1).to_broadcast([P, ITEMS, 64]),
                                             hi[:].unsqueeze(2).to_broadcast([P, ITEMS, 64]), ALU.is_equal))
            step.settle()
            nc.vector.tensor_scalar(hi_val[:, :, 0, :], hi_hot[:], lane[:, 0:1], None, ALU.mult)
            nc.vector.tensor_tensor(hi_val[:, :, 1, :], hi_hot[:],
                                    ramp[:, 0:ITEMS].unsqueeze(2).to_broadcast([P, ITEMS, 64]),
                                    ALU.mult).then_inc(hi_ready, 1)
            with dve.Fori(0, ITEMS // 8) as it:
                for t in range(8):
                    j = it * 8 + t
                    last = nc.vector.tensor_scalar(lo_hot[:, j, :], ramp[:], lo[:, bass.ds(j, 1)], None, ALU.is_equal)
                last.then_inc(lo_ready, 1)
            dve.wait_ge(listed, 1)
            step.end(nc.vector.tensor_copy(part[:].rearrange("p a h -> p (a h)"), mid_ps[0][:, 0:2 * ITEMS]))
            step.settle()
            step.end(nc.vector.scalar_tensor_tensor(item[:], part[:, 1, :], float(P), part[:, 0, :], ALU.mult, ALU.add))
            step.settle()
            nc.vector.tensor_copy(item_u[:], item[:])
            step.end(nc.vector.tensor_scalar(second[:], item[:], float(N), -float(N), ALU.is_ge, ALU.mult))
            step.settle()
            nc.vector.tensor_tensor(token_u[:], item[:], second[:], ALU.add).then_inc(list_ready, 1)

            dve.wait_ge(gap_exp, 1)
            step.end(nc.vector.tensor_scalar(wsum[:], gap[:], 1.0, None, ALU.add))
            step.settle()
            step.end(nc.vector.reciprocal(weight[:, 0, :], wsum[:]))
            step.settle()
            nc.vector.tensor_tensor(weight[:, 1, :], gap[:], weight[:, 0, :], ALU.mult)

            dve.sem_inc(y_ready, 2)
            dve.sem_inc(base_ready, 1)
            with dve.Fori(0, E // 2) as it:
                for s in range(2):
                    e = it * 2 + s
                    for a in range(2):
                        b = it * 4 + (2 * s + a)
                        nc.vector.tensor_copy(k_s[a][:], qk_t[32:32 + HS, bass.ds(b * T, T)])
                        nc.vector.tensor_tensor(v_s[a][:], lv[:, bass.ds(b * BT, BT), E:E + HS],
                                                v_bias[:].unsqueeze(1).to_broadcast([P, BT, HS]),
                                                ALU.add).then_inc(kv_ready, 1)
                    for a in range(2):
                        dve.wait_ge(wei_done, it * 4 + (2 * s + a + 1))
                        nc.vector.tensor_tensor(wei_s[a][:], wei_ps[:, 0:3 * P],
                                                causal[:].rearrange("p a t -> p (a t)"), ALU.mult).then_inc(wei_ready, 1)
                    for c in range(2):
                        n = it * 4 + (2 * s + c + 1)
                        dve.wait_ge(y_t_done, n)
                        nc.vector.tensor_copy(y_t[:, c, :], y_ps[c][:]).then_inc(y_t_ready, 1)
                        dve.wait_ge(heads_done, n)
                        nc.vector.tensor_copy(att_s[c][0:HS, :], att_ps[0:HS, 0:T]).then_inc(heads_ready, 1)
                        dve.wait_ge(y_turned, n)
                        dve.wait_ge(y_free, it * 2 + (s + 1))
                        nc.vector.tensor_copy(y_s[s][:, c * HT:(c + 1) * HT, :].rearrange("p t d -> p (t d)"),
                                              turn_ps[c][:]).then_inc(y_ready, 1)
                        dve.wait_ge(att_done, n)
                        b = it * 4 + (2 * s + c)
                        nc.vector.tensor_tensor(base[:, bass.ds(b * BT, BT), :],
                                                att_ps[:, T:2 * T].rearrange("p (t d) -> p t d", t=BT),
                                                x_all[:, bass.ds(b * BT, BT), :], ALU.add).then_inc(base_ready, 1)

            start = step.count
            with dve.Fori(0, NG // 4) as it:
                step.base = it * 4
                for s in range(4):
                    g = it * 4 + s
                    dve.wait_ge(y_back, it * 4 + (s + 1))
                    for k in range(2):
                        for t in range(TG):
                            i = g * TG + t
                            last = nc.vector.scalar_tensor_tensor(base[:, bass.ds(i, 1), :].squeeze(1), y_in[:, s, k, t, :],
                                                                  weight[:, k, bass.ds(i, 1)],
                                                                  base[:, bass.ds(i, 1), :].squeeze(1), ALU.mult, ALU.add)
                        if k == 0:
                            step.end(last)
                            step.settle()
                    last.then_inc(combined, 1)
                assert step.count == start + 4

        @block.tensor
        def _(pe):
            pe.wait_ge(consts, 1)
            pe.wait_ge(w_in_in, 64)
            pe.transpose(turn_ps[0][:, 0:80], w_in[:], ident[0:80, 0:80]).then_inc(w_in_turned, 1)
            pe.wait_ge(proj_summed, 1)
            pe.transpose(turn_ps[1][0:HS, 0:P], proj_sum[:], ident[:]).then_inc(proj_turned, 1)
            pe.wait_ge(w_in_ready, 1)
            pe.wait_ge(proj_ready, 1)

            with pe.Fori(0, NG // 4) as it:
                for pair in range(2):
                    for s in range(2):
                        g = it * 4 + (2 * pair + s)
                        pe.wait_ge(xn_ready, g + 1)
                        for t in range(TG):
                            last = pe.transpose(turn_ps[s][:, t * P:(t + 1) * P], xn[:, 2 * pair + s, t, :], ident[:])
                        last.then_inc(xn_turned, 1)
                    for s in range(2):
                        g = it * 4 + (2 * pair + s)
                        pe.wait_ge(xn_t_ready, g + 1)
                        pe.wait_ge(front_out, g * 2 + 1)
                        for t in range(TG):
                            last = pe.matmul(y_ps[s][:, t * 16:(t + 1) * 16], xn_t[:, s, t * P:(t + 1) * P],
                                             w_in_t[:, 64:80], start=True, stop=True)
                        last.then_inc(lv_done, 1)
                        pe.wait_ge(front_out, g * 2 + 2)
                        pe.matmul(mid_ps[s][0:32 + HS, :], w_in_t[:, 0:32 + HS], xn_t[:, s, :],
                                  start=True, stop=True).then_inc(qk_done, 1)

            pe.wait_ge(consts, 2)
            pe.wait_ge(chosen_ready, 1)
            pe.matmul(wei_ps[:, 0:NT * E], not_before[:], chosen[:], start=True, stop=True)
            pe.matmul(att_ps[:, 0:NT * E], ones[:], chosen[:], start=True, stop=True).then_inc(counted, 1)
            pe.wait_ge(hi_ready, 1)

            def list_items(j, n, start, stop):
                pe.wait_ge(lo_ready, n)
                for t in range(8):
                    last = pe.matmul(mid_ps[0][:, 0:2 * ITEMS], lo_hot[:, bass.ds(j + t, 1), :].squeeze(1),
                                     hi_val[:, bass.ds(j + t, 1), :, :].rearrange("p o a h -> p (o a h)"),
                                     start=start and t == 0, stop=stop and t == 7)
                return last

            list_items(0, 1, True, False)
            with pe.Fori(1, ITEMS // 8 - 1) as it:
                list_items(it * 8, it + 1, False, False)
            list_items(ITEMS - 8, ITEMS // 8, False, True).then_inc(listed, 1)

            with pe.Fori(0, E // 2) as it:
                for s in range(2):
                    def so_far(n):
                        return it * 4 + (2 * s + n)

                    def turn_rows(c):
                        pe.wait_ge(y_ready, so_far(c + 1))
                        pe.wait_ge(gathered[s][c], it * (16 * HT) + 16 * HT)
                        for t in range(HT):
                            last = pe.transpose(turn_ps[c][:, t * P:(t + 1) * P], rows_s[s][:, c * HT + t, :], ident[:])
                        last.then_inc(rows_turned, 1)

                    def up(c):
                        pe.wait_ge(rows_t_ready, so_far(c + 1))
                        for f in range(FC):
                            if f >= 2:
                                pe.wait_ge(mid_ready, it * (4 * FC) + (2 * FC * s + FC * c + f - 1))
                            pe.matmul(mid_ps[f % 2][:], w1_s[s][:, f * P:(f + 1) * P], rows_t[:, c, :],
                                      start=True, stop=True).then_inc(mid_done, 1)

                    def down(c):
                        for f in range(FC):
                            pe.wait_ge(mid_ready, it * (4 * FC) + (2 * FC * s + FC * c + f + 1))
                            last = pe.matmul(y_ps[c][:], w2_s[s][:, f, :], mid[:, f, :], start=f == 0, stop=f == FC - 1)
                        last.then_inc(y_t_done, 1)

                    def turn_y(c):
                        pe.wait_ge(y_t_ready, so_far(c + 1))
                        for t in range(HT):
                            last = pe.transpose(turn_ps[c][:, t * P:(t + 1) * P], y_t[:, c, t * P:(t + 1) * P], ident[:])
                        last.then_inc(y_turned, 1)

                    def scores(a):
                        b = it * 4 + (2 * s + a)
                        pe.wait_ge(kv_ready, so_far(a + 1))
                        if a:
                            pe.wait_ge(wei_ready, so_far(a))
                        pe.matmul(wei_ps[:, 0:T], k_s[a][:, 0:P], qk_t[0:HS, bass.ds(b * T, T)], start=True, stop=True)
                        pe.matmul(wei_ps[:, T:T + P], k_s[a][:, P:T], qk_t[0:HS, bass.ds(b * T + P, P)],
                                  start=True, stop=True).then_inc(wei_done, 1)

                    def heads(a):
                        pe.wait_ge(wei_ready, so_far(a + 1))
                        pe.wait_ge(base_ready, so_far(a + 1))
                        pe.matmul(att_ps[0:HS, 0:T], v_s[a][:, 0, :], wei_s[a][:, 0:T], start=True, stop=False)
                        pe.matmul(att_ps[0:HS, P:T], v_s[a][:, 1, :], wei_s[a][:, T:T + P],
                                  start=False, stop=True).then_inc(heads_done, 1)

                    def project(a):
                        pe.wait_ge(heads_ready, so_far(a + 1))
                        for t in range(BT):
                            last = pe.matmul(att_ps[:, T + t * P:T + (t + 1) * P], att_s[a][:, t * P:(t + 1) * P],
                                             proj_t[:], start=True, stop=True)
                        last.then_inc(att_done, 1)

                    turn_rows(0)
                    turn_rows(1)
                    scores(0)
                    pe.wait_ge(w_loaded[s], it * 32 + 32)
                    up(0)
                    scores(1)
                    down(0)
                    heads(0)
                    up(1)
                    turn_y(0)
                    project(0)
                    down(1)
                    heads(1)
                    turn_y(1)
                    project(1)


_INS = ["L0_attn_ids", "L0_attn_qkv_w", "L0_attn_qkv_b", "L0_attn_proj_w", "L0_attn_proj_b",
        "L0_ffn_router_w", "L0_ffn_w1", "L0_ffn_w2"]


def kernel(**inputs):
    import numpy as np
    import concourse.bacc as bacc
    from concourse.bass_utils import run_bass_kernel_spmd

    nc = bacc.Bacc("TRN2", target_bir_lowering=False, num_devices=1)
    arrays, args = {}, []
    for name in _INS:
        a = np.ascontiguousarray(inputs[name])
        arrays[f"in_{name}"] = a
        args.append(nc.dram_tensor(f"in_{name}", a.shape, mybir.dt.from_np(a.dtype), kind="ExternalInput").ap())
    shape = inputs["L0_attn_ids"].shape
    result = nc.dram_tensor("out_rows", shape, F32, kind="ExternalOutput").ap()
    layer_program(nc, *args, result)
    run = run_bass_kernel_spmd(nc, [arrays], core_ids=[0])
    return run.results[0]["out_rows"]
```

```python
from contextlib import ExitStack

import concourse.bass as bass
from concourse import mybir

ALU = mybir.AluOpType
ACT = mybir.ActivationFunctionType
AX = mybir.AxisListType
F32 = mybir.dt.float32
BF16 = mybir.dt.bfloat16
I32 = mybir.dt.int32
U32 = mybir.dt.uint32

P = 128
EPS = 1e-5
FILL = -3.0e38


class Steps:

    def __init__(self, engine, semaphore):
        self.engine, self.semaphore, self.count, self.base = engine, semaphore, 0, 0

    def end(self, instruction):
        instruction.then_inc(self.semaphore, 1)
        self.count += 1

    def settle(self):
        self.engine.wait_ge(self.semaphore, self.base + self.count)


def layer_program(nc, ids, qkv_w, qkv_b, proj_w, proj_b, router_w, w1, w2, out):
    B, T, D = ids.shape
    HS = qkv_w.shape[0] // 3
    NH = D // HS
    KROW, VROW, RROW = 32, 64, 72
    ROWS = RROW + router_w.shape[0]
    E, _, FF = w1.shape
    N = B * T
    NT = N // P
    TG = 4
    NG = NT // TG
    ITEMS = 2 * NT
    CT = ITEMS // E
    HALF = 512
    HT = HALF // P
    PLACES = 2 * N // P
    EARLY = 2 * CT
    RAMP = 16
    FC = FF // P
    BT = T // P
    PAIRS = B // 2
    assert D == P and T == 2 * P and NG == E and PAIRS == NG and B == 2 * E and CT * P == 2 * HALF and HS == 8 and E == 8

    x_rows = ids.rearrange("b t d -> (b t) d").rearrange("(i p) d -> p i d", p=P)
    out_rows = out.rearrange("b t d -> (b t) d").rearrange("(i p) d -> p i d", p=P)
    xn_dram = nc.dram_tensor("xn_scratch", [N, D], F32).ap()
    xn_rows = xn_dram.rearrange("(i p) d -> p i d", p=P)
    y_dram = nc.dram_tensor("y_scratch", [2 * N, D], F32).ap()
    y_rows = y_dram.rearrange("(k i p) d -> p k i d", k=2, p=P)
    w1_rows = w1.rearrange("e d f -> d e f")
    w2_rows = w2.rearrange("e (c p) d -> p e c d", p=P)

    with ExitStack() as ctx:
        def sb(name, shape, dt=F32):
            return ctx.enter_context(nc.sbuf_tensor(name, shape, dt))

        def sem(name):
            return ctx.enter_context(nc.semaphore(name))

        bank = [ctx.enter_context(nc.psum_tensor(f"bank{n}", [P, 512], F32)) for n in range(8)]
        turn_ps, mid_ps, y_ps, back_ps = bank[0:2], bank[2:4], bank[4:6], bank[6:8]

        x_all = sb("x_all", [P, NT, D])
        base = sb("base", [P, NT, D])
        qkv_t = sb("qkv_t", [P, N])
        logits = sb("logits", [P, NT, E])
        stats = sb("stats", [P, 2, TG, 6])
        mv = sb("mv", [P, 2, TG, 2])
        eps = sb("eps", [P, TG])
        var_eps = sb("var_eps", [P, 2, TG])
        power = sb("power", [P, TG])
        rstd = sb("rstd", [P, 2, TG])
        xn = sb("xn", [P, 2, TG, D])
        xn_t = sb("xn_t", [P, 2, TG * P])
        w_in = sb("w_in", [P, D])
        w_in_t = sb("w_in_t", [P, P])
        in_bias = sb("in_bias", [P, 1])
        proj_in = sb("proj_in", [P, D])
        proj_sum = sb("proj_sum", [P, HS])
        proj_t = sb("proj_t", [P, D])
        out_bias = sb("out_bias", [P, D])
        ident = sb("ident", [P, P])
        not_before = sb("not_before", [P, P], BF16)
        ones = sb("ones", [P, P], BF16)
        lane = sb("lane", [P, 1])
        item_tile = sb("item_tile", [P, ITEMS], BF16)
        prefer = sb("prefer", [P, E])
        best = sb("best", [P, 2, NT])
        hit = sb("hit", [P, 2, NT, E])
        hit_rank = sb("hit_rank", [P, NT])
        choice = sb("choice", [P, 2, NT, E])
        rest = sb("rest", [P, NT, E])
        chosen = sb("chosen", [P, E * NT], BF16)
        through = sb("through", [P, E * NT])
        place = sb("place", [P, E * NT])
        zeros = sb("zeros", [P, E * NT])
        pos = sb("pos", [P, ITEMS])
        pos_i = sb("pos_i", [P, ITEMS], I32)
        lo_i = sb("lo_i", [P, ITEMS], I32)
        hi_i = sb("hi_i", [P, ITEMS], I32)
        lo = sb("lo", [P, ITEMS], BF16)
        hi = sb("hi", [P, ITEMS], BF16)
        late = sb("late", [P, 2 * NT * D])
        y_in = late[:].rearrange("p (k i d) -> p k i d", k=2, i=NT)
        ramp = late[:, 0:P * ITEMS // 2].bitcast(BF16).rearrange("p (h j) -> p h j", j=ITEMS)
        lo_hot = late[:, P * ITEMS // 2:P * ITEMS].bitcast(BF16).rearrange("p (h j) -> p h j", j=ITEMS)
        hi_hot = sb("hi_hot", [P, PLACES, ITEMS], BF16)
        hi_val = sb("hi_val", [P, 2, PLACES, ITEMS], BF16)
        part = sb("part", [P, 2, PLACES])
        item = sb("item", [P, PLACES])
        second = sb("second", [P, PLACES])
        item_u = sb("item_u", [P, PLACES], U32)
        token_u = sb("token_u", [P, PLACES], U32)
        gap = sb("gap", [P, NT])
        weight = sb("weight", [P, 2, NT])
        wsum = sb("wsum", [P, NT])
        w1_s = [sb(f"w1_s{s}", [P, FF]) for s in range(2)]
        w2_s = [sb(f"w2_s{s}", [P, FC, D]) for s in range(2)]
        token_s = [sb(f"token_s{s}", [P, CT], U32) for s in range(2)]
        item_s = [sb(f"item_s{s}", [P, CT], U32) for s in range(2)]
        rows_s = [sb(f"rows_s{s}", [P, CT, D]) for s in range(2)]
        rows_t = sb("rows_t", [P, 2, HALF])
        mid = sb("mid", [P, FC, HALF])
        y_t = sb("y_t", [P, 2, HALF])
        y_s = [sb(f"y_s{s}", [P, CT, D]) for s in range(2)]
        k_s = [sb(f"k_s{s}", [P, 2 * T]) for s in range(2)]
        v_s = [sb(f"v_s{s}", [P, 2 * T]) for s in range(2)]
        vp_s = [sb(f"vp_s{s}", [P, 2 * BT, D]) for s in range(2)]
        wei_s = [[sb(f"wei_s{s}{a}", [P, 3 * P]) for a in range(2)] for s in range(2)]

        x_in = [sem(f"x_in{g}") for g in range(NG)]
        x_ready = sem("x_ready")
        w_in_zero = sem("w_in_zero")
        bias_zero = sem("bias_zero")
        w_in_in = sem("w_in_in")
        small_in = sem("small_in")
        proj_loaded = sem("proj_loaded")
        consts = sem("consts")
        pool_step = sem("pool_step")
        dve_step = sem("dve_step")
        held = sem("held")
        held_pe = sem("held_pe")
        mv_ready = sem("mv_ready")
        var_ready = sem("var_ready")
        rstd_ready = sem("rstd_ready")
        xn_ready = sem("xn_ready")
        xn_stored = [sem(f"xn_stored{s}") for s in range(2)]
        w_in_turned = sem("w_in_turned")
        w_in_ready = sem("w_in_ready")
        proj_summed = sem("proj_summed")
        proj_turned = sem("proj_turned")
        proj_ready = sem("proj_ready")
        xn_turned = sem("xn_turned")
        xn_t_ready = sem("xn_t_ready")
        logits_done = sem("logits_done")
        logits_ready = sem("logits_ready")
        qkv_done = sem("qkv_done")
        qkv_ready = sem("qkv_ready")
        kv_in = [sem(f"kv_in{s}") for s in range(2)]
        chosen_ready = sem("chosen_ready")
        counted = sem("counted")
        gap_ready = sem("gap_ready")
        gap_exp = sem("gap_exp")
        hot_ready = sem("hot_ready")
        listed = sem("listed")
        list_ready = sem("list_ready")
        w_loaded = [sem(f"w_loaded{s}") for s in range(2)]
        gathered = [[sem(f"gathered{s}{c}") for c in range(2)] for s in range(2)]
        scattered = [sem(f"scattered{s}") for s in range(2)]
        rows_turned = sem("rows_turned")
        rows_t_ready = sem("rows_t_ready")
        mid_done = sem("mid_done")
        mid_ready = sem("mid_ready")
        y_t_done = sem("y_t_done")
        y_t_ready = sem("y_t_ready")
        y_turned = sem("y_turned")
        y_ready = sem("y_ready")
        y_free = sem("y_free")
        ramp_start = sem("ramp_start")
        kv_zero = sem("kv_zero")
        proj_zero = sem("proj_zero")
        wei_done = sem("wei_done")
        wei_out = sem("wei_out")
        wei_ready = sem("wei_ready")
        vp_done = sem("vp_done")
        vp_ready = sem("vp_ready")
        att_done = sem("att_done")
        att_out = sem("att_out")
        x_added = sem("x_added")
        scaled = sem("scaled")
        weights_ready = sem("weights_ready")
        out_bias_in = sem("out_bias_in")
        combined = sem("combined")
        out_stored = sem("out_stored")

        block = ctx.enter_context(nc.Block())

        @block.sync
        def _(sp):
            for g in range(NG // 2):
                sp.dma_start(x_all[:, g * TG:(g + 1) * TG, :], x_rows[:, g * TG:(g + 1) * TG, :]).then_inc(x_in[g], 16)

            def keys_values(i, p):
                at = i * (2 * T)
                sp.dma_start(k_s[p][0:HS, :], qkv_t[KROW:KROW + HS, bass.ds(at, 2 * T)]).then_inc(kv_in[p], 16)
                sp.dma_start(v_s[p][0:HS, :], qkv_t[VROW:VROW + HS, bass.ds(at, 2 * T)]).then_inc(kv_in[p], 16)

            sp.wait_ge(kv_zero, 4)
            for s in range(2):
                sp.sem_inc(xn_stored[s], 16)
            AHEAD = 5
            for g in range(-AHEAD, NG):
                if g + AHEAD < NG:
                    sp.wait_ge(x_in[g + AHEAD], 16)
                    sp.sem_inc(x_ready, 1)
                if g >= 0:
                    sp.wait_ge(xn_ready, g + 1)
                    sp.dma_start(xn_rows[:, g * TG:(g + 1) * TG, :], xn[:, g % 2, :, :]).then_inc(xn_stored[g % 2], 16)
                if g in (3, 4):
                    sp.wait_ge(qkv_ready, g - 2)
                    keys_values(g - 3, g - 3)
            for s in range(2):
                sp.dma_start(w1_s[s][:], w1_rows[:, s, :]).then_inc(w_loaded[s], 16)
                sp.dma_start(w2_s[s][:], w2_rows[:, s, :, :]).then_inc(w_loaded[s], 16)
            sp.wait_ge(qkv_ready, NG)
            with sp.Fori(1, PAIRS // 2) as j:
                for p in range(2):
                    sp.wait_ge(vp_done, j * 2 + (p - 1))
                    keys_values(j * 2 + p, p)
            with sp.Fori(0, E // 2 - 1) as it:
                for s in range(2):
                    e = it * 2 + (2 + s)
                    sp.wait_ge(y_t_done, it * 4 + (2 + 2 * s))
                    sp.dma_start(w1_s[s][:], w1_rows[:, bass.ds(e, 1), :]).then_inc(w_loaded[s], 16)
                    sp.dma_start(w2_s[s][:], w2_rows[:, bass.ds(e, 1), :, :]).then_inc(w_loaded[s], 16)
            for s in range(2):
                sp.wait_ge(scattered[s], 16 * CT * E // 2)
            for g in range(NG):
                for k in range(2):
                    sp.dma_start(y_in[:, k, g * TG:(g + 1) * TG, :],
                                 y_rows[:, k, g * TG:(g + 1) * TG, :]).then_inc(x_in[g], 16)
            for g in range(NG):
                sp.wait_ge(combined, g + 1)
                sp.dma_start(out_rows[:, g * TG:(g + 1) * TG, :], base[:, g * TG:(g + 1) * TG, :]).then_inc(out_stored, 16)
            sp.wait_ge(out_stored, 16 * NG)

        @block.gpsimd
        def _(pool):
            step = Steps(pool, pool_step)
            nc.gpsimd.memset(w_in[:], 0.0).then_inc(w_in_zero, 1)
            nc.gpsimd.memset(in_bias[:], 0.0).then_inc(bias_zero, 1)
            nc.gpsimd.memset(power[:], -0.5)
            nc.gpsimd.memset(eps[:], EPS)
            step.end(nc.gpsimd.memset(ident[:], 0.0))
            step.settle()
            nc.gpsimd.affine_select(out=ident[:], in_=ident[:], compare_op=ALU.not_equal, fill=1.0, base=0,
                                    pattern=[[-1, P]], channel_multiplier=1).then_inc(consts, 1)
            nc.gpsimd.iota(ramp[:, 0:RAMP, :], [[1, RAMP], [0, ITEMS]], base=0, channel_multiplier=0,
                           allow_small_or_imprecise_dtypes=True).then_inc(ramp_start, 1)
            for s in range(2):
                nc.gpsimd.memset(k_s[s][:], 0.0).then_inc(kv_zero, 1)
                nc.gpsimd.memset(v_s[s][:], 0.0).then_inc(kv_zero, 1)
            nc.gpsimd.memset(proj_t[:], 0.0).then_inc(proj_zero, 1)
            with pool.Fori(0, NG // 2) as it:
                for s in range(2):
                    g = it * 2 + s
                    pool.wait_ge(mv_ready, g + 1)
                    nc.gpsimd.tensor_tensor(var_eps[:, s, :], mv[:, s, :, 1], eps[:], ALU.add).then_inc(var_ready, 1)
                    pool.wait_ge(var_ready, g + 1)
                    nc.gpsimd.tensor_tensor(rstd[:, s, :], var_eps[:, s, :], power[:], ALU.pow).then_inc(rstd_ready, 1)
            nc.gpsimd.memset(not_before[:], -1.0)
            nc.gpsimd.memset(ones[:], 1.0)
            nc.gpsimd.memset(zeros[:], 0.0)
            nc.gpsimd.iota(item_tile[:], [[1, ITEMS]], base=0, channel_multiplier=0, allow_small_or_imprecise_dtypes=True)
            nc.gpsimd.iota(lane[:], [[0, 1]], base=0, channel_multiplier=1, allow_small_or_imprecise_dtypes=True)
            step.end(nc.gpsimd.iota(prefer[:], [[-1, E]], base=E, channel_multiplier=0,
                                    allow_small_or_imprecise_dtypes=True))
            step.settle()
            nc.gpsimd.affine_select(out=not_before[:], in_=not_before[:], compare_op=ALU.is_ge, fill=0.0,
                                    base=0, pattern=[[-1, P]], channel_multiplier=1).then_inc(consts, 1)

            def mask(i, p):
                for a in range(2):
                    pool.wait_ge(wei_out, i * 2 + (a + 1))
                    pool.sem_inc(held, 1)
                    diagonal = wei_s[p][a][:].rearrange("p (b t) -> p b t", t=P)[:, 0:3:2, :]
                    nc.gpsimd.affine_select(out=diagonal, in_=diagonal, compare_op=ALU.is_ge, fill=0.0, base=0,
                                            pattern=[[0, 2], [1, P]], channel_multiplier=-1).then_inc(wei_ready, 1)

            with pool.Fori(0, PAIRS // 2 - 1) as j:
                for p in range(2):
                    mask(j * 2 + p, p)
            pool.sem_inc(y_free, 2)

            def take_tokens(e, s):
                step.end(nc.gpsimd.tensor_copy(token_s[s][:], token_u[:, bass.ds(e * CT, CT)]))
                step.settle()
                pool.sem_inc(held, 1)

            def gather(s, first=0, end=CT):
                for t in range(first, end):
                    nc.gpsimd.indirect_dma_start(
                        out=rows_s[s][:, t, :], out_offset=None, in_=xn_dram,
                        in_offset=bass.IndirectOffsetOnAxis(ap=token_s[s][:, t:t + 1], axis=0),
                    ).then_inc(gathered[s][t // HT], 16)

            def scatter(e, s):
                step.end(nc.gpsimd.tensor_copy(item_s[s][:], item_u[:, bass.ds(e * CT, CT)]))
                step.settle()
                for c in range(2):
                    pool.wait_ge(y_ready, e * 2 + (c + 3))
                    pool.sem_inc(held, 1)
                    for t in range(c * HT, (c + 1) * HT):
                        nc.gpsimd.indirect_dma_start(
                            out=y_dram, out_offset=bass.IndirectOffsetOnAxis(ap=item_s[s][:, t:t + 1], axis=0),
                            in_=y_s[s][:, t, :], in_offset=None,
                        ).then_inc(scattered[s], 16)

            pool.wait_ge(list_ready, 1)
            for s in range(2):
                pool.wait_ge(xn_stored[s], 16 * (NG // 2 + 1))
            take_tokens(0, 0)
            gather(0, 0, 3)
            mask(PAIRS - 2, 0)
            gather(0, 3, 7)
            mask(PAIRS - 1, 1)
            gather(0, 7, CT)
            take_tokens(1, 1)
            gather(1)
            pool.wait_ge(list_ready, 2)

            def exchange(e, s):
                pool.wait_ge(rows_turned, e * 2 + 2)
                take_tokens(e + 2, s)
                gather(s)

            def confirm(s, count):
                pool.wait_ge(scattered[s], count * (16 * CT))
                pool.sem_inc(y_free, 1)

            exchange(0, 0)
            scatter(0, 0)
            start = step.count
            with pool.Fori(0, (E - 4) // 2) as it:
                step.base = it * 4
                for s in (1, 0):
                    e = it * 2 + (2 - s)
                    exchange(e, s)
                    confirm(1 - s, it + 1)
                    scatter(e, s)
                assert step.count == start + 4
            step.base, step.count = 0, start + 4 * ((E - 4) // 2)
            exchange(E - 3, 1)
            confirm(0, E // 2 - 1)
            scatter(E - 3, 1)
            confirm(1, E // 2 - 1)
            scatter(E - 2, 0)
            scatter(E - 1, 1)

        @block.scalar
        def _(act):
            act.wait_ge(w_in_zero, 1)
            act.dma_start(w_in[0:HS, :], qkv_w[0:HS, :]).then_inc(w_in_in, 16)
            act.dma_start(w_in[KROW:KROW + HS, :], qkv_w[HS:2 * HS, :]).then_inc(w_in_in, 16)
            act.dma_start(w_in[VROW:VROW + HS, :], qkv_w[2 * HS:3 * HS, :]).then_inc(w_in_in, 16)
            act.dma_start(w_in[RROW:ROWS, :], router_w).then_inc(w_in_in, 16)
            for g in range(NG // 2, NG):
                act.dma_start(x_all[:, g * TG:(g + 1) * TG, :], x_rows[:, g * TG:(g + 1) * TG, :]).then_inc(x_in[g], 16)
            act.wait_ge(bias_zero, 1)
            act.dma_start(in_bias[0:HS, :], qkv_b[0:HS].unsqueeze(1)).then_inc(small_in, 16)
            act.dma_start(in_bias[KROW:KROW + HS, :], qkv_b[HS:2 * HS].unsqueeze(1)).then_inc(small_in, 16)
            act.dma_start(in_bias[VROW:VROW + HS, :], qkv_b[2 * HS:3 * HS].unsqueeze(1)).then_inc(small_in, 16)
            act.sem_inc(att_out, 2)

            def xn_t_out(g, s):
                act.wait_ge(xn_turned, g + 3)
                nc.scalar.copy(xn_t[:, s, :], turn_ps[s][:]).then_inc(xn_t_ready, 1)

            def features_out(g, s):
                act.wait_ge(logits_done, g + 1)
                nc.scalar.copy(logits[:, bass.ds(g * TG, TG), :],
                               y_ps[s][:, 0:TG * E].rearrange("p (t c) -> p t c", t=TG)).then_inc(logits_ready, 1)
                act.wait_ge(qkv_done, g + 1)
                nc.scalar.activation(qkv_t[:, bass.ds(g * (TG * P), TG * P)], mid_ps[s][:],
                                     ACT.Identity, bias=in_bias[:, 0:1]).then_inc(qkv_ready, 1)

            xn_t_out(0, 0)
            act.dma_start(proj_in[:], proj_w).then_inc(proj_loaded, 16)
            act.dma_start(out_bias[:], proj_b.unsqueeze(0).to_broadcast([P, D])).then_inc(out_bias_in, 16)
            act.wait_ge(small_in, 48)
            with act.Fori(0, NG // 2 - 1) as it:
                for s in range(2):
                    g = it * 2 + s
                    xn_t_out(g + 1, 1 - s)
                    features_out(g, s)
            xn_t_out(NG - 1, 1)
            features_out(NG - 2, 0)
            features_out(NG - 1, 1)
            act.wait_ge(proj_turned, 1)
            act.wait_ge(proj_zero, 1)
            nc.scalar.copy(proj_t[0:HS, :], back_ps[0][0:HS, 0:P]).then_inc(proj_ready, 1)

            def scores_out(i, p):
                for a in range(2):
                    act.wait_ge(wei_done, i * 2 + (a + 1))
                    nc.scalar.copy(wei_s[p][a][:], turn_ps[a][:, 0:3 * P]).then_inc(wei_out, 1)

            def values_out(i, p):
                act.wait_ge(vp_done, i + 1)
                nc.scalar.copy(vp_s[p][:].rearrange("p t d -> p (t d)"), mid_ps[p][:]).then_inc(vp_ready, 1)

            def attention_out(i, p):
                for a in range(2):
                    act.wait_ge(att_done, i * 2 + (a + 1))
                    nc.scalar.copy(base[:, bass.ds(i * (2 * BT) + a * BT, BT), :],
                                   y_ps[a][:, 0:BT * D].rearrange("p (t d) -> p t d", t=BT)).then_inc(att_out, 1)

            scores_out(0, 0)
            values_out(0, 0)
            with act.Fori(0, PAIRS // 2 - 1) as j:
                for p in range(2):
                    i = j * 2 + p
                    scores_out(i + 1, 1 - p)
                    values_out(i + 1, 1 - p)
                    attention_out(i, p)
            scores_out(PAIRS - 1, 1)
            values_out(PAIRS - 1, 1)
            attention_out(PAIRS - 2, 0)
            attention_out(PAIRS - 1, 1)

            act.wait_ge(gap_ready, 1)
            nc.scalar.activation(gap[:], gap[:], ACT.Exp).then_inc(gap_exp, 1)

            with act.Fori(0, E) as e:
                for c in range(2):
                    for f in range(FC):
                        act.wait_ge(mid_done, e * (2 * FC) + (c * FC + f + 1))
                        nc.scalar.activation(mid[:, f, :], mid_ps[f % 2][:], ACT.Gelu).then_inc(mid_ready, 1)

            act.wait_ge(weights_ready, 1)
            for g in range(NG):
                act.wait_ge(x_in[g], 48)
                for i in range(g * TG, (g + 1) * TG):
                    last = nc.scalar.activation(y_in[:, 0, i, :], y_in[:, 0, i, :], ACT.Copy, scale=weight[:, 0, i:i + 1])
                last.then_inc(scaled, 1)

        @block.vector
        def _(dve):
            step = Steps(dve, dve_step)

            def statistics(g, s):
                dve.wait_ge(x_ready, g + 1)
                for t in range(TG):
                    nc.vector.bn_stats(stats[:, s, t, :], x_all[:, bass.ds(g * TG + t, 1), :].squeeze(1))
                dve.drain()
                for t in range(TG):
                    last = nc.vector.bn_aggr(mv[:, s, t, :], stats[:, s, t, :])
                last.then_inc(mv_ready, 1)

            def normalise(g, s, it):
                dve.wait_ge(rstd_ready, g + 1)
                dve.wait_ge(xn_stored[s], it * 16 + 16)
                dve.wait_ge(xn_turned, g + 1)
                for t in range(TG):
                    last = nc.vector.tensor_scalar(xn[:, s, t, :], x_all[:, bass.ds(g * TG + t, 1), :].squeeze(1),
                                                   mv[:, s, t, 0:1], rstd[:, s, t:t + 1], ALU.subtract, ALU.mult)
                last.then_inc(xn_ready, 1)

            statistics(0, 0)
            dve.wait_ge(w_in_turned, 1)
            nc.vector.tensor_copy(w_in_t[:], mid_ps[0][:, 0:P]).then_inc(w_in_ready, 1)
            with dve.Fori(0, NG // 2 - 1) as it:
                for s in range(2):
                    g = it * 2 + s
                    statistics(g + 1, 1 - s)
                    normalise(g, s, it)
            dve.wait_ge(proj_loaded, 16)
            nc.vector.tensor_reduce(proj_sum[:], proj_in[:].rearrange("c (h d) -> c d h", h=NH), AX.X,
                                    ALU.add).then_inc(proj_summed, 1)
            statistics(NG - 1, 1)
            normalise(NG - 2, 0, NG // 2 - 1)
            normalise(NG - 1, 1, NG // 2 - 1)

            dve.wait_ge(ramp_start, 1)
            n = RAMP
            while n < P:
                step.end(nc.vector.tensor_scalar(ramp[:, n:2 * n, :], ramp[:, 0:n, :], float(n), None, ALU.add))
                step.settle()
                n *= 2

            dve.wait_ge(consts, 2)
            dve.wait_ge(logits_ready, NG)
            per_token = [P, NT, E]
            for k, left in enumerate((logits[:], rest[:])):
                step.end(nc.vector.tensor_reduce(best[:, k, :], left, AX.X, ALU.max))
                step.settle()
                step.end(nc.vector.tensor_tensor(hit[:, k, :, :], left,
                                                 best[:, k, :].unsqueeze(2).to_broadcast(per_token), ALU.is_equal))
                step.settle()
                step.end(nc.vector.tensor_tensor(hit[:, k, :, :], hit[:, k, :, :],
                                                 prefer[:].unsqueeze(1).to_broadcast(per_token), ALU.mult))
                step.settle()
                step.end(nc.vector.tensor_reduce(hit_rank[:], hit[:, k, :, :], AX.X, ALU.max))
                step.settle()
                step.end(nc.vector.tensor_tensor(choice[:, k, :, :], hit[:, k, :, :],
                                                 hit_rank[:].unsqueeze(2).to_broadcast(per_token), ALU.is_equal))
                step.settle()
                if k == 0:
                    step.end(nc.vector.scalar_tensor_tensor(rest[:], choice[:, 0, :, :], FILL, logits[:], ALU.mult,
                                                            ALU.add))
                    step.settle()
            nc.vector.tensor_tensor(chosen[:].rearrange("p (e i) -> p i e", e=E), choice[:, 0, :, :],
                                    choice[:, 1, :, :], ALU.add).then_inc(chosen_ready, 1)
            nc.vector.tensor_tensor(gap[:], best[:, 1, :], best[:, 0, :], ALU.subtract).then_inc(gap_ready, 1)

            dve.wait_ge(counted, 1)
            step.end(nc.vector.tensor_tensor_scan(through[:], back_ps[1][:, 0:NT * E], zeros[:], 0.0, ALU.add, ALU.add))
            step.settle()
            step.end(nc.vector.tensor_tensor(place[:], through[:], back_ps[0][:, 0:NT * E], ALU.add))
            step.settle()
            by_expert = place[:].rearrange("p (e i) -> p i e", e=E)
            for k in range(2):
                step.end(nc.vector.tensor_tensor(hit[:, k, :, :], choice[:, k, :, :], by_expert, ALU.mult))
            step.settle()
            step.end(nc.vector.tensor_reduce(pos[:], hit[:].rearrange("p k i e -> p (k i) e"), AX.X, ALU.add))
            step.settle()
            step.end(nc.vector.tensor_copy(pos_i[:], pos[:]))
            step.settle()
            nc.vector.tensor_scalar(lo_i[:], pos_i[:], P - 1, None, ALU.bitwise_and)
            step.end(nc.vector.tensor_scalar(hi_i[:], pos_i[:], 7, None, ALU.logical_shift_right))
            step.settle()
            nc.vector.tensor_copy(lo[:], lo_i[:])
            step.end(nc.vector.tensor_copy(hi[:], hi_i[:]))
            step.settle()

            def high_parts(a, b):
                n = b - a
                hot = hi_hot[:, a:b, :]
                step.end(nc.vector.tensor_tensor(hot, ramp[:, a:b, :], hi[:].unsqueeze(1).to_broadcast([P, n, ITEMS]),
                                                 ALU.is_equal))
                step.settle()
                nc.vector.tensor_scalar(hi_val[:, 0, a:b, :], hot, lane[:, 0:1], None, ALU.mult)
                return nc.vector.tensor_tensor(hi_val[:, 1, a:b, :], hot,
                                               item_tile[:].unsqueeze(1).to_broadcast([P, n, ITEMS]), ALU.mult)

            def list_out(a, b, ps):
                n = b - a
                step.end(nc.vector.tensor_copy(part[:, :, a:b], ps[:, 0:2 * n].rearrange("p (v h) -> p v h", v=2)))
                step.settle()
                step.end(nc.vector.scalar_tensor_tensor(item[:, a:b], part[:, 1, a:b], float(P), part[:, 0, a:b],
                                                        ALU.mult, ALU.add))
                step.settle()
                nc.vector.tensor_copy(item_u[:, a:b], item[:, a:b])
                step.end(nc.vector.tensor_scalar(second[:, a:b], item[:, a:b], float(N), -float(N), ALU.is_ge, ALU.mult))
                step.settle()
                nc.vector.tensor_tensor(token_u[:, a:b], item[:, a:b], second[:, a:b], ALU.add).then_inc(list_ready, 1)

            high_parts(0, EARLY)
            for k in range(2):
                items = slice(k * NT, (k + 1) * NT)
                nc.vector.tensor_tensor(lo_hot[:, :, items], ramp[:, :, items],
                                        lo[:, items].unsqueeze(1).to_broadcast([P, P, NT]), ALU.is_equal).then_inc(hot_ready, 1)
            dve.wait_ge(listed, 1)
            list_out(0, EARLY, back_ps[0])
            high_parts(EARLY, PLACES).then_inc(hot_ready, 1)
            dve.wait_ge(listed, 2)
            list_out(EARLY, PLACES, back_ps[1])

            dve.sem_inc(y_ready, 2)

            def rows_out(e, c):
                dve.wait_ge(rows_turned, e * 2 + (c + 1))
                nc.vector.tensor_copy(rows_t[:, c, :], turn_ps[c][:]).then_inc(rows_t_ready, 1)

            def expert(e, s, more):
                part_of_base = base[:, bass.ds(e * TG, TG), :]
                nc.vector.tensor_tensor(part_of_base, part_of_base, x_all[:, bass.ds(e * TG, TG), :],
                                        ALU.add).then_inc(x_added, 1)
                for c in range(2):
                    dve.wait_ge(y_t_done, e * 2 + (c + 1))
                    nc.vector.tensor_copy(y_t[:, c, :], y_ps[c][:]).then_inc(y_t_ready, 1)
                    if c == 1 and more:
                        rows_out(e + 1, 0)
                        rows_out(e + 1, 1)
                    if c == 1:
                        dve.wait_ge(x_added, e + 1)
                        nc.vector.tensor_tensor(part_of_base, part_of_base,
                                                out_bias[:].unsqueeze(1).to_broadcast([P, TG, D]), ALU.add)
                    dve.wait_ge(y_turned, e * 2 + (c + 1))
                    dve.wait_ge(y_free, e + 1)
                    nc.vector.tensor_copy(y_s[s][:, c * HT:(c + 1) * HT, :].rearrange("p t d -> p (t d)"),
                                          back_ps[c][:]).then_inc(y_ready, 1)

            rows_out(0, 0)
            rows_out(0, 1)
            dve.wait_ge(att_out, B + 2)
            dve.wait_ge(out_bias_in, 16)
            with dve.Fori(0, E // 2 - 1) as it:
                for s in range(2):
                    expert(it * 2 + s, s, True)
            expert(E - 2, 0, True)
            expert(E - 1, 1, False)

            dve.wait_ge(gap_exp, 1)
            step.end(nc.vector.tensor_scalar(wsum[:], gap[:], 1.0, None, ALU.add))
            step.settle()
            step.end(nc.vector.reciprocal(weight[:, 0, :], wsum[:]))
            step.settle()
            nc.vector.tensor_tensor(weight[:, 1, :], gap[:], weight[:, 0, :], ALU.mult).then_inc(weights_ready, 1)
            dve.wait_ge(weights_ready, 1)
            for g in range(NG):
                part_of_base = base[:, g * TG:(g + 1) * TG, :]
                dve.wait_ge(x_in[g], 48)
                for i in range(g * TG, (g + 1) * TG):
                    last = nc.vector.scalar_tensor_tensor(base[:, i, :], y_in[:, 1, i, :], weight[:, 1, i:i + 1],
                                                          base[:, i, :], ALU.mult, ALU.add)
                step.end(last)
                step.settle()
                dve.wait_ge(scaled, g + 1)
                nc.vector.tensor_tensor(part_of_base, part_of_base, y_in[:, 0, g * TG:(g + 1) * TG, :],
                                        ALU.add).then_inc(combined, 1)

        @block.tensor
        def _(pe):
            pe.wait_ge(consts, 1)

            def keep_busy(count):
                with pe.Fori(0, count):
                    pe.matmul(back_ps[1][:, 0:P], ident[:], ident[:], start=True, stop=True)

            keep_busy(10)
            pe.wait_ge(w_in_in, 64)
            pe.transpose(mid_ps[0][:, 0:P], w_in[:], ident[:]).then_inc(w_in_turned, 1)
            pe.sem_inc(xn_turned, 2)

            def turn_group(g, s):
                pe.wait_ge(xn_ready, g + 1)
                for t in range(TG):
                    last = pe.transpose(turn_ps[s][:, t * P:(t + 1) * P], xn[:, s, t, :], ident[:])
                last.then_inc(xn_turned, 1)

            def features(g, s):
                pe.wait_ge(xn_t_ready, g + 1)
                for t in range(TG):
                    last = pe.matmul(y_ps[s][:, t * E:(t + 1) * E], xn_t[:, s, t * P:(t + 1) * P],
                                     w_in_t[:, RROW:ROWS], start=True, stop=True)
                last.then_inc(logits_done, 1)
                pe.matmul(mid_ps[s][:], w_in_t[:], xn_t[:, s, :],
                          start=True, stop=True).then_inc(qkv_done, 1)

            keep_busy(8)
            turn_group(0, 0)
            pe.wait_ge(w_in_ready, 1)
            with pe.Fori(0, NG // 2 - 1) as it:
                for s in range(2):
                    g = it * 2 + s
                    turn_group(g + 1, 1 - s)
                    features(g, s)
            turn_group(NG - 1, 1)
            features(NG - 2, 0)
            pe.wait_ge(proj_summed, 1)
            pe.transpose(back_ps[0][0:HS, 0:P], proj_sum[:], ident[:]).then_inc(proj_turned, 1)
            features(NG - 1, 1)

            def scores(i, p, j):
                pe.wait_ge(kv_in[p], j * 32 + 32)
                for a in range(2):
                    at = i * (2 * T) + a * T
                    keys = k_s[p][:, a * T:(a + 1) * T]
                    pe.matmul(turn_ps[a][:, 0:T], keys[:, 0:P], qkv_t[:, bass.ds(at, T)], start=True, stop=True)
                    pe.matmul(turn_ps[a][:, T:T + P], keys[:, P:T], qkv_t[:, bass.ds(at + P, P)],
                              start=True, stop=True).then_inc(wei_done, 1)

            def project_values(i, p):
                for t in range(2 * BT):
                    last = pe.matmul(mid_ps[p][:, t * D:(t + 1) * D], v_s[p][:, t * P:(t + 1) * P], proj_t[:],
                                     start=True, stop=True)
                last.then_inc(vp_done, 1)

            def weigh_values(i, p):
                pe.wait_ge(vp_ready, i + 1)
                for a in range(2):
                    pe.wait_ge(wei_ready, i * 2 + (a + 1))
                    pe.wait_ge(att_out, i * 2 + (a + 1))
                    wei, values = wei_s[p][a], vp_s[p]
                    pe.matmul(y_ps[a][:, 0:D], wei[:, 0:P], values[:, a * BT, :], start=True, stop=True)
                    pe.matmul(y_ps[a][:, D:2 * D], wei[:, P:T], values[:, a * BT, :], start=True, stop=False)
                    pe.matmul(y_ps[a][:, D:2 * D], wei[:, T:T + P], values[:, a * BT + 1, :],
                              start=False, stop=True).then_inc(att_done, 1)

            def attention(i, p, j):
                pe.wait_ge(wei_out, i * 2 + 2)
                scores(i + 1, 1 - p, j + p)
                project_values(i + 1, 1 - p)
                weigh_values(i, p)

            def more_attention(first, end):
                with pe.Fori(first, end) as j:
                    for p in range(2):
                        attention(j * 2 + p, p, j)

            def list_items(a, b, ps):
                for t in range(ITEMS):
                    if a == 0 and t % NT == 0:
                        pe.wait_ge(hot_ready, t // NT + 1)
                    last = pe.matmul(ps[:, 0:2 * (b - a)], lo_hot[:, :, t], hi_val[:, :, a:b, t],
                                     start=t == 0, stop=t == ITEMS - 1)
                last.then_inc(listed, 1)

            pe.wait_ge(qkv_ready, NG)
            scores(0, 0, 0)
            pe.wait_ge(proj_ready, 1)
            project_values(0, 0)
            attention(0, 0, 0)
            pe.wait_ge(chosen_ready, 1)
            pe.matmul(back_ps[0][:, 0:NT * E], not_before[:], chosen[:], start=True, stop=True)
            pe.matmul(back_ps[1][:, 0:NT * E], ones[:], chosen[:], start=True, stop=True).then_inc(counted, 1)
            attention(1, 1, 0)
            more_attention(1, 2)
            list_items(0, EARLY, back_ps[0])
            more_attention(2, PAIRS // 2 - 1)
            pe.wait_ge(wei_out, 2 * (PAIRS - 1))
            scores(PAIRS - 1, 1, PAIRS // 2 - 1)
            project_values(PAIRS - 1, 1)
            pe.wait_ge(hot_ready, 3)
            list_items(EARLY, PLACES, back_ps[1])
            weigh_values(PAIRS - 2, 0)
            weigh_values(PAIRS - 1, 1)

            def turn_rows(e, s, c, it):
                pe.wait_ge(gathered[s][c], it * (16 * HT) + 16 * HT)
                for t in range(HT):
                    last = pe.transpose(turn_ps[c][:, t * P:(t + 1) * P], rows_s[s][:, c * HT + t, :], ident[:])
                last.then_inc(rows_turned, 1)

            def up(e, s, c):
                pe.wait_ge(rows_t_ready, e * 2 + (c + 1))
                for f in range(FC):
                    if f >= 2:
                        pe.wait_ge(mid_ready, e * (2 * FC) + (FC * c + f - 1))
                    pe.matmul(mid_ps[f % 2][:], w1_s[s][:, f * P:(f + 1) * P], rows_t[:, c, :],
                              start=True, stop=True).then_inc(mid_done, 1)

            def down(e, s, c):
                for f in range(FC):
                    pe.wait_ge(mid_ready, e * (2 * FC) + (FC * c + f + 1))
                    last = pe.matmul(y_ps[c][:], w2_s[s][:, f, :], mid[:, f, :], start=f == 0, stop=f == FC - 1)
                last.then_inc(y_t_done, 1)

            def turn_back(e, s, c):
                pe.wait_ge(y_t_ready, e * 2 + (c + 1))
                pe.wait_ge(y_ready, e * 2 + (c + 1))
                for t in range(HT):
                    last = pe.transpose(back_ps[c][:, t * P:(t + 1) * P], y_t[:, c, t * P:(t + 1) * P], ident[:])
                last.then_inc(y_turned, 1)

            def expert(e, s, it, more):
                pe.wait_ge(w_loaded[s], it * 32 + 32)
                up(e, s, 0)
                down(e, s, 0)
                up(e, s, 1)
                turn_back(e, s, 0)
                down(e, s, 1)
                if more:
                    for c in range(2):
                        turn_rows(e + 1, 1 - s, c, it + s)
                turn_back(e, s, 1)

            for c in range(2):
                turn_rows(0, 0, c, 0)
            pe.wait_ge(att_out, B + 2)
            with pe.Fori(0, E // 2 - 1) as it:
                for s in range(2):
                    expert(it * 2 + s, s, it, True)
            expert(E - 2, 0, E // 2 - 1, True)
            expert(E - 1, 1, E // 2 - 1, False)


_INS = ["L0_attn_ids", "L0_attn_qkv_w", "L0_attn_qkv_b", "L0_attn_proj_w", "L0_attn_proj_b",
        "L0_ffn_router_w", "L0_ffn_w1", "L0_ffn_w2"]


def kernel(**inputs):
    import numpy as np
    import concourse.bacc as bacc
    from concourse.bass_utils import run_bass_kernel_spmd

    nc = bacc.Bacc("TRN2", target_bir_lowering=False, num_devices=1)
    arrays, args = {}, []
    for name in _INS:
        a = np.ascontiguousarray(inputs[name])
        arrays[f"in_{name}"] = a
        args.append(nc.dram_tensor(f"in_{name}", a.shape, mybir.dt.from_np(a.dtype), kind="ExternalInput").ap())
    shape = inputs["L0_attn_ids"].shape
    result = nc.dram_tensor("out_rows", shape, F32, kind="ExternalOutput").ap()
    layer_program(nc, *args, result)
    run = run_bass_kernel_spmd(nc, [arrays], core_ids=[0])
    return run.results[0]["out_rows"]
```

```python
from contextlib import ExitStack

import concourse.bass as bass
from concourse import mybir

ALU = mybir.AluOpType
ACT = mybir.ActivationFunctionType
AX = mybir.AxisListType
F32 = mybir.dt.float32
BF16 = mybir.dt.bfloat16
I32 = mybir.dt.int32
U32 = mybir.dt.uint32

P = 128
EPS = 1e-5
FILL = -3.0e38


class Steps:

    def __init__(self, engine, semaphore):
        self.engine, self.semaphore, self.count, self.base = engine, semaphore, 0, 0

    def end(self, instruction):
        instruction.then_inc(self.semaphore, 1)
        self.count += 1

    def settle(self):
        self.engine.wait_ge(self.semaphore, self.base + self.count)


def layer_program(nc, ids, qkv_w, qkv_b, proj_w, proj_b, router_w, w1, w2, out):
    B, T, D = ids.shape
    HS = qkv_w.shape[0] // 3
    NH = D // HS
    KROW, VROW, RROW = 32, 64, 72
    ROWS = RROW + router_w.shape[0]
    E, _, FF = w1.shape
    N = B * T
    NT = N // P
    TG = 4
    NG = NT // TG
    ITEMS = 2 * NT
    CT = ITEMS // E
    HALF = 512
    HT = HALF // P
    PLACES = 2 * N // P
    EARLY = 2 * CT
    RAMP = 16
    BANKS = 4
    HOTS = ITEMS // 4
    FC = FF // P
    BT = T // P
    PAIRS = B // 2
    assert D == P and T == 2 * P and NG == E and PAIRS == NG and B == 2 * E
    assert CT * P == 2 * HALF and HS == 8 and E == 8

    x_rows = ids.rearrange("b t d -> (b t) d").rearrange("(i p) d -> p i d", p=P)
    out_rows = out.rearrange("b t d -> (b t) d").rearrange("(i p) d -> p i d", p=P)
    xn_dram = nc.dram_tensor("xn_scratch", [N, D], F32).ap()
    xn_rows = xn_dram.rearrange("(i p) d -> p i d", p=P)
    y_dram = nc.dram_tensor("y_scratch", [2 * N, D], F32).ap()
    y_rows = y_dram.rearrange("(k i p) d -> p k i d", k=2, p=P)
    w1_rows = w1.rearrange("e d f -> d e f")
    w2_rows = w2.rearrange("e (c p) d -> p e c d", p=P)

    with ExitStack() as ctx:
        def sb(name, shape, dt=F32):
            return ctx.enter_context(nc.sbuf_tensor(name, shape, dt))

        def sem(name):
            return ctx.enter_context(nc.semaphore(name))

        bank = [ctx.enter_context(nc.psum_tensor(f"bank{n}", [P, 512], F32)) for n in range(8)]
        turn_ps, mid_ps, y_ps, back_ps = bank[0:2], bank[2:4], bank[4:6], bank[6:8]

        x_all = sb("x_all", [P, NT, D])
        base = sb("base", [P, NT, D])
        qkv_t = sb("qkv_t", [P, N])
        logits = sb("logits", [P, NT, E])
        stats = sb("stats", [P, 2, TG, 6])
        mv = sb("mv", [P, 2, TG, 2])
        eps = sb("eps", [P, TG])
        var_eps = sb("var_eps", [P, 2, TG])
        power = sb("power", [P, TG])
        rstd = sb("rstd", [P, 2, TG])
        xn = sb("xn", [P, 2, TG, D])
        xn_t = sb("xn_t", [P, 2, TG * P])
        w_in = sb("w_in", [P, D])
        w_in_t = sb("w_in_t", [P, P])
        in_bias = sb("in_bias", [P, 1])
        proj_in = sb("proj_in", [P, D])
        proj_sum = sb("proj_sum", [P, HS])
        proj_t = sb("proj_t", [P, D])
        out_bias = sb("out_bias", [P, D])
        ident = sb("ident", [P, P])
        not_before = sb("not_before", [P, P], BF16)
        ones = sb("ones", [P, P], BF16)
        lane = sb("lane", [P, 1])
        item_tile = sb("item_tile", [P, ITEMS], BF16)
        prefer = sb("prefer", [P, E])
        best = sb("best", [P, 2, NT])
        hit = sb("hit", [P, 2, NT, E])
        hit_rank = sb("hit_rank", [P, NT])
        choice = sb("choice", [P, 2, NT, E])
        rest = sb("rest", [P, NT, E])
        chosen = sb("chosen", [P, E * NT], BF16)
        through = sb("through", [P, E * NT])
        place = sb("place", [P, E * NT])
        zeros = sb("zeros", [P, E * NT])
        pos = sb("pos", [P, ITEMS])
        pos_i = sb("pos_i", [P, ITEMS], I32)
        lo_i = sb("lo_i", [P, ITEMS], I32)
        hi_i = sb("hi_i", [P, ITEMS], I32)
        lo = sb("lo", [P, ITEMS], BF16)
        hi = sb("hi", [P, ITEMS], BF16)
        late = sb("late", [P, 2 * NT * D])
        y_in = late[:].rearrange("p (k i d) -> p k i d", k=2, i=NT)
        ramp = late[:, 0:P * ITEMS // 2].bitcast(BF16).rearrange("p (h j) -> p h j", j=ITEMS)
        lo_hot = late[:, P * ITEMS // 2:P * ITEMS].bitcast(BF16).rearrange("p (h j) -> p h j", j=ITEMS)
        hi_hot = sb("hi_hot", [P, PLACES, ITEMS], BF16)
        hi_val = sb("hi_val", [P, 2, PLACES, ITEMS], BF16)
        part = sb("part", [P, 2, PLACES])
        item = sb("item", [P, PLACES])
        second = sb("second", [P, PLACES])
        item_u = sb("item_u", [P, PLACES], U32)
        token_u = sb("token_u", [P, PLACES], U32)
        gap = sb("gap", [P, NT])
        weight = sb("weight", [P, 2, NT])
        wsum = sb("wsum", [P, NT])
        w1_s = [sb(f"w1_s{s}", [P, FF]) for s in range(2)]
        w2_s = [sb(f"w2_s{s}", [P, FC, D]) for s in range(2)]
        token_s = [sb(f"token_s{s}", [P, CT], U32) for s in range(2)]
        item_s = [sb(f"item_s{s}", [P, CT], U32) for s in range(2)]
        rows_s = [sb(f"rows_s{s}", [P, CT, D]) for s in range(2)]
        rows_t = sb("rows_t", [P, 2, HALF])
        mid = sb("mid", [P, 2, FC, HALF])
        y_s = [sb(f"y_s{s}", [P, CT, D]) for s in range(2)]
        k_s = [sb(f"k_s{s}", [P, 2 * T]) for s in range(2)]
        v_s = [sb(f"v_s{s}", [P, 2 * T]) for s in range(2)]
        vp_s = [sb(f"vp_s{s}", [P, 2 * BT, D]) for s in range(2)]
        wei_s = [[sb(f"wei_s{s}{a}", [P, 3 * P]) for a in range(2)] for s in range(2)]

        x_in = [sem(f"x_in{g}") for g in range(NG)]
        x_ready = sem("x_ready")
        w_in_zero = sem("w_in_zero")
        bias_zero = sem("bias_zero")
        w_in_in = sem("w_in_in")
        small_in = sem("small_in")
        proj_loaded = sem("proj_loaded")
        consts = sem("consts")
        pool_step = sem("pool_step")
        dve_step = sem("dve_step")
        held = sem("held")
        mv_ready = sem("mv_ready")
        var_ready = sem("var_ready")
        rstd_ready = sem("rstd_ready")
        xn_ready = sem("xn_ready")
        xn_stored = [sem(f"xn_stored{s}") for s in range(2)]
        w_in_turned = sem("w_in_turned")
        w_in_ready = sem("w_in_ready")
        proj_summed = sem("proj_summed")
        proj_turned = sem("proj_turned")
        proj_ready = sem("proj_ready")
        xn_turned = sem("xn_turned")
        xn_t_ready = sem("xn_t_ready")
        logits_done = sem("logits_done")
        logits_ready = sem("logits_ready")
        qkv_done = sem("qkv_done")
        qkv_ready = sem("qkv_ready")
        kv_in = [sem(f"kv_in{s}") for s in range(2)]
        chosen_ready = sem("chosen_ready")
        counted = sem("counted")
        gap_ready = sem("gap_ready")
        gap_exp = sem("gap_exp")
        hot_ready = sem("hot_ready")
        listed = sem("listed")
        list_ready = sem("list_ready")
        w_loaded = [sem(f"w_loaded{s}") for s in range(2)]
        gathered = [[sem(f"gathered{s}{c}") for c in range(2)] for s in range(2)]
        tokens_ready = sem("tokens_ready")
        items_ready = sem("items_ready")
        scattered = [sem(f"scattered{s}") for s in range(2)]
        rows_turned = sem("rows_turned")
        rows_t_ready = sem("rows_t_ready")
        mid_done = sem("mid_done")
        mid_ready = sem("mid_ready")
        y_done = sem("y_done")
        y_ready = sem("y_ready")
        y_free = sem("y_free")
        ramp_start = sem("ramp_start")
        kv_zero = sem("kv_zero")
        proj_zero = sem("proj_zero")
        wei_done = sem("wei_done")
        wei_out = sem("wei_out")
        wei_ready = sem("wei_ready")
        vp_done = sem("vp_done")
        vp_ready = sem("vp_ready")
        att_done = sem("att_done")
        att_out = sem("att_out")
        x_added = sem("x_added")
        scaled = sem("scaled")
        weights_ready = sem("weights_ready")
        out_bias_in = sem("out_bias_in")
        second_added = sem("second_added")
        combined = sem("combined")
        last_combined = sem("last_combined")
        out_stored = sem("out_stored")

        block = ctx.enter_context(nc.Block())

        @block.sync
        def _(sp):
            for g in range(NG // 2):
                sp.dma_start(x_all[:, g * TG:(g + 1) * TG, :], x_rows[:, g * TG:(g + 1) * TG, :]).then_inc(x_in[g], 16)

            def keys_values(i, p):
                at = i * (2 * T)
                sp.dma_start(k_s[p][0:HS, :], qkv_t[KROW:KROW + HS, bass.ds(at, 2 * T)]).then_inc(kv_in[p], 16)
                sp.dma_start(v_s[p][0:HS, :], qkv_t[VROW:VROW + HS, bass.ds(at, 2 * T)]).then_inc(kv_in[p], 16)

            for s in range(2):
                sp.sem_inc(xn_stored[s], 16)
            AHEAD = 5
            for g in range(-AHEAD, NG):
                if g + AHEAD < NG:
                    sp.wait_ge(x_in[g + AHEAD], 16)
                    sp.sem_inc(x_ready, 1)
                if g >= 0:
                    sp.wait_ge(xn_ready, g + 1)
                    sp.dma_start(xn_rows[:, g * TG:(g + 1) * TG, :], xn[:, g % 2, :, :]).then_inc(xn_stored[g % 2], 16)
                if g == 3:
                    sp.wait_ge(kv_zero, 4)
                if g in (3, 4):
                    sp.wait_ge(qkv_ready, g - 2)
                    keys_values(g - 3, g - 3)
            for s in range(2):
                sp.dma_start(w1_s[s][:], w1_rows[:, s, :]).then_inc(w_loaded[s], 16)
                sp.dma_start(w2_s[s][:], w2_rows[:, s, :, :]).then_inc(w_loaded[s], 16)
            sp.wait_ge(qkv_ready, NG)
            with sp.Fori(1, PAIRS // 2) as j:
                for p in range(2):
                    sp.wait_ge(vp_done, j * 2 + (p - 1))
                    keys_values(j * 2 + p, p)
            with sp.Fori(0, E // 2 - 1) as it:
                for s in range(2):
                    e = it * 2 + (2 + s)
                    sp.wait_ge(y_done, it * (2 * CT) + (s + 1) * CT)
                    sp.dma_start(w1_s[s][:], w1_rows[:, bass.ds(e, 1), :]).then_inc(w_loaded[s], 16)
                    sp.dma_start(w2_s[s][:], w2_rows[:, bass.ds(e, 1), :, :]).then_inc(w_loaded[s], 16)
            for s in range(2):
                sp.wait_ge(scattered[s], 16 * CT * E // 2)
            for g in range(NG):
                for k in range(2):
                    sp.dma_start(y_in[:, k, g * TG:(g + 1) * TG, :],
                                 y_rows[:, k, g * TG:(g + 1) * TG, :]).then_inc(x_in[g], 16)
            for g in range(NG):
                if g < NG - 1:
                    sp.wait_ge(combined, g + 1)
                else:
                    sp.wait_ge(last_combined, 1)
                sp.dma_start(out_rows[:, g * TG:(g + 1) * TG, :], base[:, g * TG:(g + 1) * TG, :]).then_inc(out_stored, 16)
            sp.wait_ge(out_stored, 16 * NG)

        @block.gpsimd
        def _(pool):
            step = Steps(pool, pool_step)
            nc.gpsimd.memset(w_in[:], 0.0).then_inc(w_in_zero, 1)
            nc.gpsimd.memset(in_bias[:], 0.0).then_inc(bias_zero, 1)
            nc.gpsimd.memset(power[:], -0.5)
            nc.gpsimd.memset(eps[:], EPS)
            step.end(nc.gpsimd.memset(ident[:], 0.0))
            step.settle()
            nc.gpsimd.affine_select(out=ident[:], in_=ident[:], compare_op=ALU.not_equal, fill=1.0, base=0,
                                    pattern=[[-1, P]], channel_multiplier=1).then_inc(consts, 1)
            nc.gpsimd.iota(ramp[:, 0:RAMP, :], [[1, RAMP], [0, ITEMS]], base=0, channel_multiplier=0,
                           allow_small_or_imprecise_dtypes=True).then_inc(ramp_start, 1)
            for s in range(2):
                nc.gpsimd.memset(k_s[s][:], 0.0).then_inc(kv_zero, 1)
                nc.gpsimd.memset(v_s[s][:], 0.0).then_inc(kv_zero, 1)
            nc.gpsimd.memset(proj_t[:], 0.0).then_inc(proj_zero, 1)
            with pool.Fori(0, NG // 2) as it:
                for s in range(2):
                    g = it * 2 + s
                    pool.wait_ge(mv_ready, g + 1)
                    nc.gpsimd.tensor_tensor(var_eps[:, s, :], mv[:, s, :, 1], eps[:], ALU.add).then_inc(var_ready, 1)
                    pool.wait_ge(var_ready, g + 1)
                    nc.gpsimd.tensor_tensor(rstd[:, s, :], var_eps[:, s, :], power[:], ALU.pow).then_inc(rstd_ready, 1)
            nc.gpsimd.memset(not_before[:], -1.0)
            nc.gpsimd.memset(ones[:], 1.0)
            nc.gpsimd.memset(zeros[:], 0.0)
            nc.gpsimd.iota(item_tile[:], [[1, ITEMS]], base=0, channel_multiplier=0, allow_small_or_imprecise_dtypes=True)
            nc.gpsimd.iota(lane[:], [[0, 1]], base=0, channel_multiplier=1, allow_small_or_imprecise_dtypes=True)
            step.end(nc.gpsimd.iota(prefer[:], [[-1, E]], base=E, channel_multiplier=0,
                                    allow_small_or_imprecise_dtypes=True))
            step.settle()
            nc.gpsimd.affine_select(out=not_before[:], in_=not_before[:], compare_op=ALU.is_ge, fill=0.0,
                                    base=0, pattern=[[-1, P]], channel_multiplier=1).then_inc(consts, 1)

            def mask(i, p):
                for a in range(2):
                    pool.wait_ge(wei_out, i * 2 + (a + 1))
                    pool.sem_inc(held, 1)
                    diagonal = wei_s[p][a][:].rearrange("p (b t) -> p b t", t=P)[:, 0:3:2, :]
                    nc.gpsimd.affine_select(out=diagonal, in_=diagonal, compare_op=ALU.is_ge, fill=0.0, base=0,
                                            pattern=[[0, 2], [1, P]], channel_multiplier=-1).then_inc(wei_ready, 1)

            with pool.Fori(0, 2) as j:
                for p in range(2):
                    mask(j * 2 + p, p)
            mask(PAIRS - 4, 0)
            pool.sem_inc(y_free, 2)

            def take_tokens(e):
                pool.wait_ge(tokens_ready, e + 1)
                pool.sem_inc(held, 1)

            def gather(s, first=0, end=CT):
                for t in range(first, end):
                    nc.gpsimd.indirect_dma_start(
                        out=rows_s[s][:, t, :], out_offset=None, in_=xn_dram,
                        in_offset=bass.IndirectOffsetOnAxis(ap=token_s[s][:, t:t + 1], axis=0),
                    ).then_inc(gathered[s][t // HT], 16)

            def scatter(e, s, wait_tiles=(HT, HT)):
                pool.wait_ge(items_ready, e + 1)
                t = 0
                for count in wait_tiles:
                    pool.wait_ge(y_ready, e * CT + (t + count + BANKS))
                    pool.sem_inc(held, 1)
                    for t in range(t, t + count):
                        nc.gpsimd.indirect_dma_start(
                            out=y_dram, out_offset=bass.IndirectOffsetOnAxis(ap=item_s[s][:, t:t + 1], axis=0),
                            in_=y_s[s][:, t, :], in_offset=None,
                        ).then_inc(scattered[s], 16)
                    t += 1

            for s in range(2):
                pool.wait_ge(xn_stored[s], 16 * (NG // 2 + 1))
            take_tokens(0)
            gather(0, 0, 2)
            mask(PAIRS - 3, 1)
            gather(0, 2)
            take_tokens(1)
            mask(PAIRS - 2, 0)
            gather(1, 0, 3)
            mask(PAIRS - 1, 1)
            gather(1, 3)

            def exchange(e, s):
                take_tokens(e + 2)
                gather(s)

            def confirm(s, count):
                pool.wait_ge(scattered[s], count * (16 * CT))
                pool.sem_inc(y_free, 1)

            exchange(0, 0)
            scatter(0, 0)
            with pool.Fori(0, (E - 4) // 2) as it:
                for s in (1, 0):
                    e = it * 2 + (2 - s)
                    exchange(e, s)
                    confirm(1 - s, it + 1)
                    scatter(e, s)
            exchange(E - 3, 1)
            confirm(0, E // 2 - 1)
            scatter(E - 3, 1)
            confirm(1, E // 2 - 1)
            scatter(E - 2, 0)
            scatter(E - 1, 1, (1,) * CT)
            for g in range(NG - 1):
                part_of_base = base[:, g * TG:(g + 1) * TG, :]
                pool.wait_ge(second_added, g + 1)
                pool.wait_ge(scaled, g + 1)
                nc.gpsimd.tensor_tensor(part_of_base, part_of_base, y_in[:, 0, g * TG:(g + 1) * TG, :],
                                        ALU.add).then_inc(combined, 1)

        @block.scalar
        def _(act):
            act.wait_ge(w_in_zero, 1)
            act.dma_start(w_in[0:HS, :], qkv_w[0:HS, :]).then_inc(w_in_in, 16)
            act.dma_start(w_in[KROW:KROW + HS, :], qkv_w[HS:2 * HS, :]).then_inc(w_in_in, 16)
            act.dma_start(w_in[VROW:VROW + HS, :], qkv_w[2 * HS:3 * HS, :]).then_inc(w_in_in, 16)
            act.dma_start(w_in[RROW:ROWS, :], router_w).then_inc(w_in_in, 16)
            for g in range(NG // 2, NG):
                act.dma_start(x_all[:, g * TG:(g + 1) * TG, :], x_rows[:, g * TG:(g + 1) * TG, :]).then_inc(x_in[g], 16)
            act.wait_ge(bias_zero, 1)
            act.dma_start(in_bias[0:HS, :], qkv_b[0:HS].unsqueeze(1)).then_inc(small_in, 16)
            act.dma_start(in_bias[KROW:KROW + HS, :], qkv_b[HS:2 * HS].unsqueeze(1)).then_inc(small_in, 16)
            act.dma_start(in_bias[VROW:VROW + HS, :], qkv_b[2 * HS:3 * HS].unsqueeze(1)).then_inc(small_in, 16)
            act.sem_inc(att_out, 2)

            def xn_t_out(g, s):
                act.wait_ge(xn_turned, g + 3)
                nc.scalar.copy(xn_t[:, s, :], turn_ps[s][:]).then_inc(xn_t_ready, 1)

            def logits_out(g, s):
                act.wait_ge(logits_done, g + 1)
                nc.scalar.copy(logits[:, bass.ds(g * TG, TG), :],
                               y_ps[s][:, 0:TG * E].rearrange("p (t c) -> p t c", t=TG)).then_inc(logits_ready, 1)

            def qkv_out(g, s):
                act.wait_ge(qkv_done, g + 1)
                nc.scalar.activation(qkv_t[:, bass.ds(g * (TG * P), TG * P)], mid_ps[s][:],
                                     ACT.Identity, bias=in_bias[:, 0:1]).then_inc(qkv_ready, 1)

            act.wait_ge(w_in_turned, 1)
            nc.scalar.copy(w_in_t[:], mid_ps[0][:, 0:P]).then_inc(w_in_ready, 1)
            xn_t_out(0, 0)
            act.dma_start(proj_in[:], proj_w).then_inc(proj_loaded, 16)
            act.dma_start(out_bias[:], proj_b.unsqueeze(0).to_broadcast([P, D])).then_inc(out_bias_in, 16)
            act.wait_ge(small_in, 48)
            with act.Fori(0, NG // 2 - 1) as it:
                for s in range(2):
                    g = it * 2 + s
                    xn_t_out(g + 1, 1 - s)
                    logits_out(g, s)
                    qkv_out(g, s)
            xn_t_out(NG - 1, 1)
            for g in (NG - 2, NG - 1):
                logits_out(g, g % 2)
            for g in (NG - 2, NG - 1):
                qkv_out(g, g % 2)
            act.wait_ge(proj_turned, 1)
            act.wait_ge(proj_zero, 1)
            nc.scalar.copy(proj_t[0:HS, :], back_ps[0][0:HS, 0:P]).then_inc(proj_ready, 1)

            def scores_out(i, p):
                for a in range(2):
                    act.wait_ge(wei_done, i * 2 + (a + 1))
                    nc.scalar.copy(wei_s[p][a][:], turn_ps[a][:, 0:3 * P]).then_inc(wei_out, 1)

            def values_out(i, p):
                act.wait_ge(vp_done, i + 1)
                nc.scalar.copy(vp_s[p][:].rearrange("p t d -> p (t d)"), mid_ps[p][:]).then_inc(vp_ready, 1)

            def attention_out(i, p):
                for a in range(2):
                    act.wait_ge(att_done, i * 2 + (a + 1))
                    nc.scalar.copy(base[:, bass.ds(i * (2 * BT) + a * BT, BT), :],
                                   y_ps[a][:, 0:BT * D].rearrange("p (t d) -> p t d", t=BT)).then_inc(att_out, 1)

            scores_out(0, 0)
            values_out(0, 0)
            with act.Fori(0, PAIRS // 2 - 1) as j:
                for p in range(2):
                    i = j * 2 + p
                    scores_out(i + 1, 1 - p)
                    values_out(i + 1, 1 - p)
                    attention_out(i, p)
            scores_out(PAIRS - 1, 1)
            values_out(PAIRS - 1, 1)
            attention_out(PAIRS - 2, 0)

            act.sem_inc(mid_ready, 2)
            with act.Fori(0, E) as e:
                for c in range(2):
                    for f in range(FC):
                        act.wait_ge(mid_done, e * (2 * FC) + (c * FC + f + 1))
                        nc.scalar.activation(mid[:, c, f, :], mid_ps[f % 2][:], ACT.Gelu).then_inc(mid_ready, 1)

            act.wait_ge(gap_ready, 1)
            nc.scalar.activation(gap[:], gap[:], ACT.Exp).then_inc(gap_exp, 1)

            act.wait_ge(weights_ready, 1)
            for g in range(NG):
                act.wait_ge(x_in[g], 48)
                for i in range(g * TG, (g + 1) * TG):
                    last = nc.scalar.activation(y_in[:, 0, i, :], y_in[:, 0, i, :], ACT.Copy, scale=weight[:, 0, i:i + 1])
                last.then_inc(scaled, 1)

        @block.vector
        def _(dve):
            step = Steps(dve, dve_step)

            def statistics(g, s):
                dve.wait_ge(x_ready, g + 1)
                for t in range(TG):
                    nc.vector.bn_stats(stats[:, s, t, :], x_all[:, bass.ds(g * TG + t, 1), :].squeeze(1))
                dve.drain()
                for t in range(TG):
                    last = nc.vector.bn_aggr(mv[:, s, t, :], stats[:, s, t, :])
                last.then_inc(mv_ready, 1)

            def normalise(g, s, it):
                dve.wait_ge(rstd_ready, g + 1)
                dve.wait_ge(xn_stored[s], it * 16 + 16)
                dve.wait_ge(xn_turned, g + 1)
                for t in range(TG):
                    last = nc.vector.tensor_scalar(xn[:, s, t, :], x_all[:, bass.ds(g * TG + t, 1), :].squeeze(1),
                                                   mv[:, s, t, 0:1], rstd[:, s, t:t + 1], ALU.subtract, ALU.mult)
                last.then_inc(xn_ready, 1)

            statistics(0, 0)
            with dve.Fori(0, NG // 2 - 1) as it:
                for s in range(2):
                    g = it * 2 + s
                    statistics(g + 1, 1 - s)
                    normalise(g, s, it)
            dve.wait_ge(proj_loaded, 16)
            nc.vector.tensor_reduce(proj_sum[:], proj_in[:].rearrange("c (h d) -> c d h", h=NH), AX.X,
                                    ALU.add).then_inc(proj_summed, 1)
            statistics(NG - 1, 1)
            normalise(NG - 2, 0, NG // 2 - 1)
            normalise(NG - 1, 1, NG // 2 - 1)

            dve.wait_ge(ramp_start, 1)
            n = RAMP
            while n < P:
                step.end(nc.vector.tensor_scalar(ramp[:, n:2 * n, :], ramp[:, 0:n, :], float(n), None, ALU.add))
                step.settle()
                n *= 2

            dve.wait_ge(consts, 2)
            dve.wait_ge(logits_ready, NG)
            per_token = [P, NT, E]
            for k, left in enumerate((logits[:], rest[:])):
                step.end(nc.vector.tensor_reduce(best[:, k, :], left, AX.X, ALU.max))
                step.settle()
                step.end(nc.vector.tensor_tensor(hit[:, k, :, :], left,
                                                 best[:, k, :].unsqueeze(2).to_broadcast(per_token), ALU.is_equal))
                step.settle()
                step.end(nc.vector.tensor_tensor(hit[:, k, :, :], hit[:, k, :, :],
                                                 prefer[:].unsqueeze(1).to_broadcast(per_token), ALU.mult))
                step.settle()
                step.end(nc.vector.tensor_reduce(hit_rank[:], hit[:, k, :, :], AX.X, ALU.max))
                step.settle()
                step.end(nc.vector.tensor_tensor(choice[:, k, :, :], hit[:, k, :, :],
                                                 hit_rank[:].unsqueeze(2).to_broadcast(per_token), ALU.is_equal))
                step.settle()
                if k == 0:
                    step.end(nc.vector.scalar_tensor_tensor(rest[:], choice[:, 0, :, :], FILL, logits[:], ALU.mult,
                                                            ALU.add))
                    step.settle()
            nc.vector.tensor_tensor(chosen[:].rearrange("p (e i) -> p i e", e=E), choice[:, 0, :, :],
                                    choice[:, 1, :, :], ALU.add).then_inc(chosen_ready, 1)
            nc.vector.tensor_tensor(gap[:], best[:, 1, :], best[:, 0, :], ALU.subtract).then_inc(gap_ready, 1)

            dve.wait_ge(counted, 1)
            step.end(nc.vector.tensor_tensor_scan(through[:], back_ps[1][:, 0:NT * E], zeros[:], 0.0, ALU.add, ALU.add))
            step.settle()
            step.end(nc.vector.tensor_tensor(place[:], through[:], back_ps[0][:, 0:NT * E], ALU.add))
            step.settle()
            by_expert = place[:].rearrange("p (e i) -> p i e", e=E)
            for k in range(2):
                step.end(nc.vector.tensor_tensor(hit[:, k, :, :], choice[:, k, :, :], by_expert, ALU.mult))
            step.settle()
            step.end(nc.vector.tensor_reduce(pos[:], hit[:].rearrange("p k i e -> p (k i) e"), AX.X, ALU.add))
            step.settle()
            step.end(nc.vector.tensor_copy(pos_i[:], pos[:]))
            step.settle()
            nc.vector.tensor_scalar(lo_i[:], pos_i[:], P - 1, None, ALU.bitwise_and)
            step.end(nc.vector.tensor_scalar(hi_i[:], pos_i[:], 7, None, ALU.logical_shift_right))
            step.settle()
            nc.vector.tensor_copy(lo[:], lo_i[:])
            step.end(nc.vector.tensor_copy(hi[:], hi_i[:]))
            step.settle()

            def high_parts(a, b):
                n = b - a
                hot = hi_hot[:, a:b, :]
                step.end(nc.vector.tensor_tensor(hot, ramp[:, a:b, :], hi[:].unsqueeze(1).to_broadcast([P, n, ITEMS]),
                                                 ALU.is_equal))
                step.settle()
                nc.vector.tensor_scalar(hi_val[:, 0, a:b, :], hot, lane[:, 0:1], None, ALU.mult)
                return nc.vector.tensor_tensor(hi_val[:, 1, a:b, :], hot,
                                               item_tile[:].unsqueeze(1).to_broadcast([P, n, ITEMS]), ALU.mult)

            def list_out(a, b, ps):
                n = b - a
                step.end(nc.vector.tensor_copy(part[:, :, a:b], ps[:, 0:2 * n].rearrange("p (v h) -> p v h", v=2)))
                step.settle()
                step.end(nc.vector.scalar_tensor_tensor(item[:, a:b], part[:, 1, a:b], float(P), part[:, 0, a:b],
                                                        ALU.mult, ALU.add))
                step.settle()
                nc.vector.tensor_copy(item_u[:, a:b], item[:, a:b])
                step.end(nc.vector.tensor_scalar(second[:, a:b], item[:, a:b], float(N), -float(N), ALU.is_ge, ALU.mult))
                step.settle()
                nc.vector.tensor_tensor(token_u[:, a:b], item[:, a:b], second[:, a:b], ALU.add).then_inc(list_ready, 1)

            def tokens(e, s):
                nc.vector.tensor_copy(token_s[s][:], token_u[:, bass.ds(e * CT, CT)]).then_inc(tokens_ready, 1)

            high_parts(0, EARLY)
            for first in range(0, ITEMS, HOTS):
                items = slice(first, first + HOTS)
                nc.vector.tensor_tensor(lo_hot[:, :, items], ramp[:, :, items],
                                        lo[:, items].unsqueeze(1).to_broadcast([P, P, HOTS]),
                                        ALU.is_equal).then_inc(hot_ready, 1)
            dve.wait_ge(listed, 1)
            list_out(0, EARLY, back_ps[0])
            dve.wait_ge(list_ready, 1)
            for s in range(2):
                tokens(s, s)
            high_parts(EARLY, PLACES).then_inc(hot_ready, 1)
            dve.wait_ge(listed, 2)
            list_out(EARLY, PLACES, back_ps[1])
            dve.wait_ge(list_ready, 2)

            def rows_out(e, c):
                dve.wait_ge(rows_turned, e * 2 + (c + 1))
                nc.vector.tensor_copy(rows_t[:, c, :], turn_ps[c][:]).then_inc(rows_t_ready, 1)

            def expert(e, s, more=True, more_tokens=True):
                if more_tokens:
                    tokens(e + 2, s)
                dve.wait_ge(y_free, e + 1)
                nc.vector.tensor_copy(item_s[s][:], item_u[:, bass.ds(e * CT, CT)]).then_inc(items_ready, 1)
                part_of_base = base[:, bass.ds(e * TG, TG), :]
                nc.vector.tensor_tensor(part_of_base, part_of_base, x_all[:, bass.ds(e * TG, TG), :],
                                        ALU.add).then_inc(x_added, 1)
                for c in range(2):
                    if more:
                        rows_out(e + 1, c)
                    for t in range(HT):
                        at = c * HT + t
                        dve.wait_ge(y_done, e * CT + (at + 1))
                        nc.vector.tensor_copy(y_s[s][:, at, :], bank[BANKS + at % BANKS][:, 0:D]).then_inc(y_ready, 1)
                dve.wait_ge(x_added, e + 1)
                nc.vector.tensor_tensor(part_of_base, part_of_base,
                                        out_bias[:].unsqueeze(1).to_broadcast([P, TG, D]), ALU.add)

            rows_out(0, 0)
            rows_out(0, 1)
            dve.wait_ge(att_out, B)
            for a in range(2):
                at = (PAIRS - 1) * (2 * BT) + a * BT
                dve.wait_ge(att_done, B - 1 + a)
                nc.vector.tensor_copy(base[:, at:at + BT, :],
                                      y_ps[a][:, 0:BT * D].rearrange("p (t d) -> p t d", t=BT)).then_inc(att_out, 1)
            dve.wait_ge(att_out, B + 2)
            dve.sem_inc(y_ready, BANKS)
            dve.wait_ge(out_bias_in, 16)
            with dve.Fori(0, E // 2 - 1) as it:
                for s in range(2):
                    expert(it * 2 + s, s)
            expert(E - 2, 0, more_tokens=False)
            expert(E - 1, 1, more=False, more_tokens=False)

            dve.wait_ge(gap_exp, 1)
            step.end(nc.vector.tensor_scalar(wsum[:], gap[:], 1.0, None, ALU.add))
            step.settle()
            step.end(nc.vector.reciprocal(weight[:, 0, :], wsum[:]))
            step.settle()
            nc.vector.tensor_tensor(weight[:, 1, :], gap[:], weight[:, 0, :], ALU.mult).then_inc(weights_ready, 1)
            dve.wait_ge(weights_ready, 1)
            for g in range(NG):
                part_of_base = base[:, g * TG:(g + 1) * TG, :]
                dve.wait_ge(x_in[g], 48)
                for i in range(g * TG, (g + 1) * TG):
                    last = nc.vector.scalar_tensor_tensor(base[:, i, :], y_in[:, 1, i, :], weight[:, 1, i:i + 1],
                                                          base[:, i, :], ALU.mult, ALU.add)
                if g < NG - 1:
                    last.then_inc(second_added, 1)
                else:
                    step.end(last)
                    step.settle()
                    dve.wait_ge(scaled, g + 1)
                    nc.vector.tensor_tensor(part_of_base, part_of_base, y_in[:, 0, g * TG:(g + 1) * TG, :],
                                            ALU.add).then_inc(last_combined, 1)

        @block.tensor
        def _(pe):
            pe.wait_ge(consts, 1)

            def keep_busy(count):
                with pe.Fori(0, count):
                    pe.matmul(back_ps[1][:, 0:P], ident[:], ident[:], start=True, stop=True)

            keep_busy(6)
            pe.wait_ge(w_in_in, 64)
            pe.transpose(mid_ps[0][:, 0:P], w_in[:], ident[:]).then_inc(w_in_turned, 1)
            pe.sem_inc(xn_turned, 2)

            def turn_group(g, s):
                pe.wait_ge(xn_ready, g + 1)
                for t in range(TG):
                    last = pe.transpose(turn_ps[s][:, t * P:(t + 1) * P], xn[:, s, t, :], ident[:])
                last.then_inc(xn_turned, 1)

            def router(g, s):
                pe.wait_ge(xn_t_ready, g + 1)
                for t in range(TG):
                    last = pe.matmul(y_ps[s][:, t * E:(t + 1) * E], xn_t[:, s, t * P:(t + 1) * P],
                                     w_in_t[:, RROW:ROWS], start=True, stop=True)
                last.then_inc(logits_done, 1)

            def queries_keys_values(s):
                pe.matmul(mid_ps[s][:], w_in_t[:], xn_t[:, s, :],
                          start=True, stop=True).then_inc(qkv_done, 1)

            keep_busy(8)
            turn_group(0, 0)
            pe.wait_ge(w_in_ready, 1)
            with pe.Fori(0, NG // 2 - 1) as it:
                for s in range(2):
                    g = it * 2 + s
                    turn_group(g + 1, 1 - s)
                    router(g, s)
                    queries_keys_values(s)
            turn_group(NG - 1, 1)
            router(NG - 2, 0)
            router(NG - 1, 1)
            queries_keys_values(0)
            pe.wait_ge(proj_summed, 1)
            pe.transpose(back_ps[0][0:HS, 0:P], proj_sum[:], ident[:]).then_inc(proj_turned, 1)
            queries_keys_values(1)

            def scores(i, p, j):
                pe.wait_ge(kv_in[p], j * 32 + 32)
                for a in range(2):
                    at = i * (2 * T) + a * T
                    keys = k_s[p][:, a * T:(a + 1) * T]
                    pe.matmul(turn_ps[a][:, 0:T], keys[:, 0:P], qkv_t[:, bass.ds(at, T)], start=True, stop=True)
                    pe.matmul(turn_ps[a][:, T:T + P], keys[:, P:T], qkv_t[:, bass.ds(at + P, P)],
                              start=True, stop=True).then_inc(wei_done, 1)

            def project_values(i, p):
                for t in range(2 * BT):
                    last = pe.matmul(mid_ps[p][:, t * D:(t + 1) * D], v_s[p][:, t * P:(t + 1) * P], proj_t[:],
                                     start=True, stop=True)
                last.then_inc(vp_done, 1)

            def weigh_values(i, p):
                pe.wait_ge(vp_ready, i + 1)
                for a in range(2):
                    pe.wait_ge(wei_ready, i * 2 + (a + 1))
                    pe.wait_ge(att_out, i * 2 + (a + 1))
                    wei, values = wei_s[p][a], vp_s[p]
                    pe.matmul(y_ps[a][:, 0:D], wei[:, 0:P], values[:, a * BT, :], start=True, stop=True)
                    pe.matmul(y_ps[a][:, D:2 * D], wei[:, P:T], values[:, a * BT, :], start=True, stop=False)
                    pe.matmul(y_ps[a][:, D:2 * D], wei[:, T:T + P], values[:, a * BT + 1, :],
                              start=False, stop=True).then_inc(att_done, 1)

            def attention(i, p, j):
                pe.wait_ge(wei_out, i * 2 + 2)
                scores(i + 1, 1 - p, j + p)
                project_values(i + 1, 1 - p)
                weigh_values(i, p)

            def list_items(a, b, ps):
                for t in range(ITEMS):
                    if a == 0 and t % HOTS == 0:
                        pe.wait_ge(hot_ready, t // HOTS + 1)
                    last = pe.matmul(ps[:, 0:2 * (b - a)], lo_hot[:, :, t], hi_val[:, :, a:b, t],
                                     start=t == 0, stop=t == ITEMS - 1)
                last.then_inc(listed, 1)

            scores(0, 0, 0)
            pe.wait_ge(qkv_ready, NG)
            pe.wait_ge(proj_ready, 1)
            project_values(0, 0)
            pe.wait_ge(wei_out, 2)
            scores(1, 1, 0)
            pe.wait_ge(chosen_ready, 1)
            pe.matmul(back_ps[0][:, 0:NT * E], not_before[:], chosen[:], start=True, stop=True)
            pe.matmul(back_ps[1][:, 0:NT * E], ones[:], chosen[:], start=True, stop=True).then_inc(counted, 1)
            project_values(1, 1)
            weigh_values(0, 0)
            attention(1, 1, 0)
            attention(2, 0, 1)
            list_items(0, EARLY, back_ps[0])

            with pe.Fori(1, PAIRS // 2 - 1) as j:
                attention(j * 2 + 1, 1, j)
                attention(j * 2 + 2, 0, j + 1)
            pe.wait_ge(hot_ready, ITEMS // HOTS + 1)
            list_items(EARLY, PLACES, back_ps[1])

            def turn_rows(e, s, c, it):
                pe.wait_ge(gathered[s][c], it * (16 * HT) + 16 * HT)
                for t in range(HT):
                    last = pe.transpose(turn_ps[c][:, t * P:(t + 1) * P], rows_s[s][:, c * HT + t, :], ident[:])
                last.then_inc(rows_turned, 1)

            def up(e, s, c):
                pe.wait_ge(rows_t_ready, e * 2 + (c + 1))
                for f in range(FC):
                    pe.wait_ge(mid_ready, e * (2 * FC) + (FC * c + f + 1))
                    pe.matmul(mid_ps[f % 2][:], w1_s[s][:, f * P:(f + 1) * P], rows_t[:, c, :],
                              start=True, stop=True).then_inc(mid_done, 1)

            def down(e, s, c):
                pe.wait_ge(mid_ready, e * (2 * FC) + (FC * (c + 1) + 2))
                for t in range(HT):
                    at = c * HT + t
                    pe.wait_ge(y_ready, e * CT + (at + 1))
                    for f in range(FC):
                        last = pe.matmul(bank[BANKS + at % BANKS][:, 0:D], mid[:, c, f, t * P:(t + 1) * P],
                                         w2_s[s][:, f, :], start=f == 0, stop=f == FC - 1)
                    last.then_inc(y_done, 1)

            def expert(e, s, it, more):
                pe.wait_ge(w_loaded[s], it * 32 + 32)
                for c in range(2):
                    up(e, s, c)
                    if more:
                        turn_rows(e + 1, 1 - s, c, it + s)
                for c in range(2):
                    down(e, s, c)

            pe.wait_ge(wei_out, 2 * PAIRS)
            for c in range(2):
                turn_rows(0, 0, c, 0)
            weigh_values(PAIRS - 1, 1)
            with pe.Fori(0, E // 2 - 1) as it:
                for s in range(2):
                    expert(it * 2 + s, s, it, True)
            expert(E - 2, 0, E // 2 - 1, True)
            expert(E - 1, 1, E // 2 - 1, False)


_INS = ["L0_attn_ids", "L0_attn_qkv_w", "L0_attn_qkv_b", "L0_attn_proj_w", "L0_attn_proj_b",
        "L0_ffn_router_w", "L0_ffn_w1", "L0_ffn_w2"]


def kernel(**inputs):
    import numpy as np
    import concourse.bacc as bacc
    from concourse.bass_utils import run_bass_kernel_spmd

    nc = bacc.Bacc("TRN2", target_bir_lowering=False, num_devices=1)
    arrays, args = {}, []
    for name in _INS:
        a = np.ascontiguousarray(inputs[name])
        arrays[f"in_{name}"] = a
        args.append(nc.dram_tensor(f"in_{name}", a.shape, mybir.dt.from_np(a.dtype), kind="ExternalInput").ap())
    shape = inputs["L0_attn_ids"].shape
    result = nc.dram_tensor("out_rows", shape, F32, kind="ExternalOutput").ap()
    layer_program(nc, *args, result)
    run = run_bass_kernel_spmd(nc, [arrays], core_ids=[0])
    return run.results[0]["out_rows"]
```
